# Optimizing a Trainium2 kernel written in Bass

```python
import numpy as np
import jax
import jax.numpy as jnp

def _softmax(x, axis=-1):
    return jax.nn.softmax(x, axis=axis)

def _gelu(x):
    return jax.nn.gelu(x, approximate=True)

def _silu(x):
    return jax.nn.silu(x)

def _sigmoid(x):
    return jax.nn.sigmoid(x)

def _layernorm(x, axis=-1, eps=1e-05):
    m = jnp.mean(x, axis=axis, keepdims=True)
    v = jnp.var(x, axis=axis, keepdims=True)
    return (x - m) / jnp.sqrt(v + eps)

def _scatter_add(tgt, idx, src, axis=0):
    return tgt.at[idx].add(src)

def _segment_sum(src, seg, n):
    return jax.ops.segment_sum(src, seg, n)
kernel_name = 'mk_xattn_seq_d1_seqx_r8_172d52'

def setup_inputs(seed: int=0):
    np.random.seed(seed)
    _w = jnp.asarray

    def _rec_inputs():
        import jax
        import jax.numpy as jnp
        _rk = jax.random.key(seed)
        x = 7.22e-05 + 1 * jax.random.normal(jax.random.fold_in(_rk, 1), (8, 100, 128), jnp.float32)
        _lenS = 100 - jax.random.randint(jax.random.fold_in(_rk, 7), (8,), 0, max(1, 100 // 4) + 1, jnp.int32)
        _lenS2 = 1444 - jax.random.randint(jax.random.fold_in(_rk, 8), (8,), 0, max(1, 1444 // 4) + 1, jnp.int32)
        _ctx_1024P = jax.random.normal(jax.random.fold_in(_rk, 11), (8, 16, 128), jnp.float32)
        _ctx_1024c = jax.random.dirichlet(jax.random.fold_in(_rk, 511), 0.3 * jnp.ones((16,), jnp.float32), (8, 1444))
        _ctx_1024t = jnp.einsum('bsk,bkd->bsd', _ctx_1024c, _ctx_1024P)
        _ctx_1024t = _ctx_1024t * jax.lax.rsqrt(jnp.mean(jnp.square(_ctx_1024t)) + 1e-12) * 0.953939
        ctx_1024 = 4.13588e-05 + 0.999923 * (_ctx_1024t + 0.3 * jax.random.normal(jax.random.fold_in(_rk, 611), (8, 1444, 128), jnp.float32))
        return (x, ctx_1024)
    x, ctx_1024 = _rec_inputs()

    def _L0_xattn_setup():
        import jax, jax.numpy as jnp
        import numpy as np
        N_HEAD, M_DIM, K_DIM, V_DIM = (16, 128, 64, 64)
        LN_EPS = 1e-05
        key = jax.random.key(seed)
        ks = jax.random.split(key, 10)
        B, L = (4, 256)
        q = jax.random.normal(ks[0], (B, L, M_DIM), dtype=jnp.float32)
        k = jax.random.normal(ks[1], (B, L, M_DIM), dtype=jnp.float32)
        v = jax.random.normal(ks[2], (B, L, M_DIM), dtype=jnp.float32)
        s = 1.0 / np.sqrt(M_DIM)
        W_qs = jax.random.normal(ks[3], (M_DIM, N_HEAD * K_DIM), dtype=jnp.float32) * s
        W_ks = jax.random.normal(ks[4], (M_DIM, N_HEAD * K_DIM), dtype=jnp.float32) * s
        W_vs = jax.random.normal(ks[5], (M_DIM, N_HEAD * V_DIM), dtype=jnp.float32) * s
        fc_w = jax.random.normal(ks[6], (N_HEAD * V_DIM, M_DIM), dtype=jnp.float32) * (1.0 / np.sqrt(N_HEAD * V_DIM))
        fc_b = jnp.zeros((M_DIM,), dtype=jnp.float32)
        ln_g = jnp.ones((M_DIM,), dtype=jnp.float32)
        ln_b = jnp.zeros((M_DIM,), dtype=jnp.float32)
        return {'q': q, 'k': k, 'v': v, 'W_qs': W_qs, 'W_ks': W_ks, 'W_vs': W_vs, 'fc_w': fc_w, 'fc_b': fc_b, 'ln_g': ln_g, 'ln_b': ln_b}
    _L0_xattn_all = _L0_xattn_setup()
    _L0_xattn_in = {k: v for k, v in _L0_xattn_all.items() if k in ('W_qs', 'W_ks', 'W_vs', 'fc_w', 'fc_b', 'ln_g', 'ln_b')}
    del _L0_xattn_all
    return {'x': x, 'ctx_1024': ctx_1024, 'L0_xattn_W_qs': _L0_xattn_in['W_qs'], 'L0_xattn_W_ks': _L0_xattn_in['W_ks'], 'L0_xattn_W_vs': _L0_xattn_in['W_vs'], 'L0_xattn_fc_w': _L0_xattn_in['fc_w'], 'L0_xattn_fc_b': _L0_xattn_in['fc_b'], 'L0_xattn_ln_g': _L0_xattn_in['ln_g'], 'L0_xattn_ln_b': _L0_xattn_in['ln_b']}

def reference(x, ctx_1024, L0_xattn_W_qs, L0_xattn_W_ks, L0_xattn_W_vs, L0_xattn_fc_w, L0_xattn_fc_b, L0_xattn_ln_g, L0_xattn_ln_b):
    import jax
    import jax.numpy as jnp

    def _L0_xattn_ref(q, k, v, W_qs, W_ks, W_vs, fc_w, fc_b, ln_g, ln_b):
        import jax, jax.numpy as jnp
        import numpy as np
        N_HEAD, M_DIM, K_DIM, V_DIM = (16, 128, 64, 64)
        LN_EPS = 1e-05
        B, Lq, _ = q.shape
        residual = q
        qh = (q @ W_qs).reshape(B, Lq, N_HEAD, K_DIM)
        kh = (k @ W_ks).reshape(B, k.shape[1], N_HEAD, K_DIM)
        vh = (v @ W_vs).reshape(B, v.shape[1], N_HEAD, V_DIM)
        temperature = np.power(K_DIM, 0.5).astype(np.float32)
        attn = jnp.einsum('bqhd,bkhd->bhqk', qh, kh) / temperature
        attn = jax.nn.softmax(attn, axis=-1)
        out = jnp.einsum('bhqk,bkhd->bqhd', attn, vh).reshape(B, Lq, N_HEAD * V_DIM)
        out = out @ fc_w + fc_b
        x = out + residual
        mu = jnp.mean(x, axis=-1, keepdims=True)
        var = jnp.mean(jnp.square(x - mu), axis=-1, keepdims=True)
        return (x - mu) * jax.lax.rsqrt(var + LN_EPS) * ln_g + ln_b
    x = _L0_xattn_ref(x, ctx_1024, ctx_1024, L0_xattn_W_qs, L0_xattn_W_ks, L0_xattn_W_vs, L0_xattn_fc_w, L0_xattn_fc_b, L0_xattn_ln_g, L0_xattn_ln_b)
    return x

_drawn_inputs = setup_inputs


def setup_inputs(seed=0):
    import zlib

    import numpy as np

    out = dict(_drawn_inputs(seed))
    spreads = {'L0_xattn_fc_b': (0.0, 0.1), 'L0_xattn_ln_g': (1.0, 0.2), 'L0_xattn_ln_b': (0.0, 0.1)}
    factors = {}
    for name, (base, spread) in spreads.items():
        noise = np.random.default_rng([zlib.crc32(name.encode()), seed]).standard_normal(out[name].shape)
        drawn = base * np.exp(spread * noise) if base else spread * noise
        out[name] = jnp.asarray(drawn.astype(out[name].dtype))
    for name, factor in factors.items():
        out[name] = (out[name] * factor).astype(out[name].dtype)
    return out
```

```python
from contextlib import ExitStack

import concourse.bass as bass
from concourse import mybir

F32 = mybir.dt.float32
F32R = mybir.dt.float32r
ALU = mybir.AluOpType
ACT = mybir.ActivationFunctionType
AX = mybir.AxisListType

P = 128
HEADS = 16
KD = 64
TEMPERATURE = float(KD) ** 0.5
LN_EPS = 1e-5

SLOTS = 12
CHUNKS = 3
CS = SLOTS // CHUNKS
QG = 4
RING = 5
TBANKS = 2
GROUPS = [range(0, 3), range(3, 6), range(6, 9), range(9, 13)]
NG = len(GROUPS)

SIDE = {3: [("q", 0)], 4: [("proj", 0)], 5: [("ctxT", 0)], 6: [("q", 1)], 8: [("ctxT", 1)], 9: [("q", 2)],
        11: [("ctxT", 2)], 12: [("q", 3)]}
NEXT = ("q", "ctxT")
PREV = ("proj",)


def cross_attention(nc, x, ctx, w_q, w_k, w_v, fc_w, fc_b, ln_g, ln_b, out):
    B, Q, D = x.shape
    K = ctx.shape[1]
    V = fc_w.shape[1]
    ROWS = HEADS * Q
    TILES = -(-ROWS // P)
    PAIRS = HEADS * KD // P
    FULL, REST = divmod(K, SLOTS)
    assert D == P and V == P and Q <= P and REST == CS and TILES == GROUPS[-1].stop

    def keys_on(c):
        return FULL + 1 if c == 0 else FULL

    WIDTH = [CS * keys_on(c) for c in range(CHUNKS)]
    START = [sum(WIDTH[:c]) for c in range(CHUNKS)]
    assert sum(WIDTH) == K and max(WIDTH) <= 512

    def rows(t):
        return min(P, ROWS - P * t)

    def group_of(t):
        return next(g for g in range(NG) if t in GROUPS[g])

    def group_rows(g):
        return sum(rows(t) for t in GROUPS[g])

    NC = CHUNKS * TILES
    QBLOCKS = HEADS // QG
    QB = QG * Q

    def q_block_of(t):
        return (P * t + rows(t) - 1) // QB

    def step_entries(t):
        scores = [("s", t + 1, c) for c in range(CHUNKS)]
        side = [(kind, t, n) for kind, n in SIDE.get(t, [])]
        return side + scores if t == TILES - 1 else scores + side

    order = [e for t in range(TILES) for e in step_entries(t)]
    short = -len(order) % RING
    rounds = [RING] * ((len(order) - short * (RING - 1)) // RING) + [RING - 1] * short
    bank_of = dict(zip(order, [bank for r in rounds for bank in range(r)], strict=True))
    early = ([("xT", n) for n in range(2)] + [("wqT", n) for n in range(2)] + [("wkT", n) for n in range(2)]
             + [("A", n) for n in range(4)] + [("ctxT", c) for c in range(CHUNKS)] + [("q", n) for n in range(4)]
             + [("s", 0, c) for c in range(CHUNKS)] + [("wvT", n) for n in range(2)] + [("M", n) for n in range(4)])
    early_bank = {e: n % RING for n, e in enumerate(early)}

    def copied(e):
        return sum(f[0] not in ("s", "q", "ctxT") for f in early[:early.index(e) + 1])

    with ExitStack() as stack:
        def sb(name, shape, dt=F32):
            return stack.enter_context(nc.sbuf_tensor(name, shape, dt))

        def sem(name):
            return stack.enter_context(nc.semaphore(name))

        ident = sb("ident", [P, P])
        recip_line = nc.dram_tensor("recip_line", [NG, 512], F32, kind="Internal").ap()
        one = sb("one", [P, 1, 1])
        ctx_in = sb("ctx_in", [P, SLOTS, P])
        ctx_hi = sb("ctx_hi", [P, SLOTS, P], F32R)
        ctx_lo = sb("ctx_lo", [P, SLOTS, P], F32R)
        ctxT_hi = sb("ctxT_hi", [P, 2, K], F32R)
        ctxT_lo = sb("ctxT_lo", [P, 2, K], F32R)
        q_hi = sb("q_hi", [P, TILES * P], F32R)
        q_lo = sb("q_lo", [P, TILES * P], F32R)
        weights = sb("weights", [P, 2, K])
        wt_hi = [sb(f"wt_hi{i}", [P, SLOTS, group_rows(2 + i)], F32R) for i in range(2)]
        wt_lo = [sb(f"wt_lo{i}", [P, SLOTS, group_rows(2 + i)], F32R) for i in range(2)]
        mx = sb("mx", [P, TILES, CHUNKS])
        neg_max = sb("neg_max", [P, TILES])
        row_sum = sb("row_sum", [P, TILES, CHUNKS])
        total = sb("total", [P, TILES])
        recip = sb("recip", [P, TILES])
        recip_rows = sb("recip_rows", [P, P * len(GROUPS[-1])])
        attended = sb("attended", [P, ROWS])
        A = sb("A", [P, HEADS, P])
        M = sb("M", [P, HEADS, P])
        xT = sb("xT", [P, B * Q])
        x_in = sb("x_in", [Q, B, P])
        x_res = sb("x_res", [Q, B, P])
        w_in = sb("w_in", [P, HEADS * KD])
        wk_in = sb("wk_in", [P, HEADS * KD])
        wT = sb("wT", [P, PAIRS, P])
        wkT = sb("wkT", [P, PAIRS, P])
        fc_in = sb("fc_in", [P, PAIRS, P])
        rows_in = sb("rows_in", [Q, 3, P])
        y = sb("y", [Q, P])
        y_sum, y_mean, squares = sb("y_sum", [Q, 1]), sb("y_mean", [Q, 1]), sb("squares", [Q, 1])
        centred = sb("centred", [Q, P])
        z = sb("z", [Q, B, P])
        var = sb("var", [Q, B])
        std = sb("std", [Q, B])
        unused = sb("unused", [Q, 1])
        rstd = sb("rstd", [Q, B])

        ring = [stack.enter_context(nc.psum_tensor(f"ring{i}", [P, 512], F32)) for i in range(RING)]
        tbank = [stack.enter_context(nc.psum_tensor(f"tbank{i}", [P, CS, P], F32)) for i in range(TBANKS)]
        pv = stack.enter_context(nc.psum_tensor("pv", [P, 512], F32))

        ident_zeroed, ident_ready = sem("ident_zeroed"), sem("ident_ready")
        filler_set = sem("filler_set")
        x_loaded, wq_loaded, wk_loaded, wv_loaded = sem("x_loaded"), sem("wq_loaded"), sem("wk_loaded"), sem("wv_loaded")
        fc_loaded, rows_loaded, ctx_loaded = sem("fc_loaded"), sem("rows_loaded"), sem("ctx_loaded")
        early_filled, early_copied = sem("early_filled"), sem("early_copied")
        x_res_ready = sem("x_res_ready")
        scores_ready = sem("scores_ready")
        chunk_max = sem("chunk_max")
        max_ready = sem("max_ready")
        exp_done = sem("exp_done")
        wt_ready = sem("wt_ready")
        wt_hi_done = sem("wt_hi_done")
        wt_lo_done = sem("wt_lo_done")
        pv_done = sem("pv_done")
        total_ready = sem("total_ready")
        recip_ready = sem("recip_ready")
        recip_stored = sem("recip_stored")
        rows_spread = sem("rows_spread")
        attended_done = sem("attended_done")
        q_ready, q_hi_done, q_lo_done = sem("q_ready"), sem("q_hi_done"), sem("q_lo_done")
        ctxT_ready, ctxT_hi_done, ctxT_lo_done = sem("ctxT_ready"), sem("ctxT_hi_done"), sem("ctxT_lo_done")
        ctx_hi_done, ctx_lo_done = sem("ctx_hi_done"), sem("ctx_lo_done")
        proj_ready = sem("proj_ready")
        y_ready, mean_ready, centred_ready = sem("y_ready"), sem("mean_ready"), sem("centred_ready")
        squares_ready, z_ready = sem("squares_ready"), sem("z_ready")
        var_ready, std_ready, rstd_ready, result_ready, stored = sem("var_ready"), sem("std_ready"), sem("rstd_ready"), sem("result_ready"), sem("stored")

        def batches(eng, body):
            body(0, True, False)
            with eng.Fori(1, B - 1) as b:
                body(b, False, False)
            body(B - 1, False, True)

        def in_batch(kind, first, last):
            return not (first and kind in PREV) and not (last and kind in NEXT)

        def side_work(t, first, last):
            return [(kind, n) for kind, n in SIDE.get(t, []) if in_batch(kind, first, last)]

        def there(e, first, last):
            if e[0] == "s":
                return not (last and e[1] == TILES)
            return in_batch(e[0], first, last)

        def read_out(e, b):
            kind, t, n = e
            if kind == "s":
                return exp_done, b * NC + (CHUNKS * t + n + 1)
            if kind == "q":
                return q_lo_done, b * QBLOCKS + (QBLOCKS + n + 1)
            if kind == "ctxT":
                return ctxT_lo_done, b * CHUNKS + (CHUNKS + n + 1)
            return y_ready, b

        def early_read_out(e):
            if e[0] in ("s", "q", "ctxT"):
                n = e[2] if e[0] == "s" else e[1]
                return {"s": exp_done, "q": q_lo_done, "ctxT": ctxT_lo_done}[e[0]], n + 1
            return early_copied, copied(e)

        def bank_free(e, b, first, last):
            bank = bank_of[e]
            before = [f for f in order[:order.index(e)] if bank_of[f] == bank and there(f, first, last)]
            if before:
                return read_out(before[-1], b)
            if first:
                return early_read_out([f for f in early if early_bank[f] == bank][-1])
            return read_out([f for f in order if bank_of[f] == bank][-1], b - 1)

        block = stack.enter_context(nc.Block())

        def load_ctx(sp, b):
            sp.dma_start(ctx_in[0:FULL, :, :],
                         ctx[b, 0:SLOTS * FULL, :].rearrange("(p s) d -> p s d", s=SLOTS)).then_inc(ctx_loaded, 16)
            sp.dma_start(ctx_in[FULL:FULL + 1, 0:CS, :],
                         ctx[b, SLOTS * FULL:K, :].rearrange("(p s) d -> p s d", s=CS)).then_inc(ctx_loaded, 16)

        @block.sync
        def _(sp):
            sp.dma_start(x_in[:, :, :], x.rearrange("b q d -> q b d")).then_inc(x_loaded, 16)
            sp.dma_start(w_in[:, :], w_q).then_inc(wq_loaded, 16)
            load_ctx(sp, 0)
            sp.dma_start(fc_in[:, :, :], fc_w.rearrange("(n p) d -> p n d", p=P)).then_inc(fc_loaded, 16)
            sp.wait_ge(early_filled, copied(("wqT", 1)))
            sp.dma_start(w_in[:, :], w_v).then_inc(wv_loaded, 16)
            def spread_reciprocals(b, g, first):
                n = len(GROUPS[g])
                sp.wait_ge(recip_ready, b * NG + g + 1)
                sp.dma_start(recip_line[g, 0:P * n].rearrange("(p t) -> p t", t=n),
                             recip[:, GROUPS[g].start:GROUPS[g].stop]).then_inc(recip_stored, 16)
                sp.wait_ge(recip_stored, b * 16 * NG + 16 * (g + 1))
                if not (first and g == 0):
                    sp.wait_ge(attended_done, b * NG + g)
                sp.dma_start(recip_rows[:, 0:P * n], recip_line[g:g + 1, 0:P * n].broadcast_to([P, P * n]))\
                  .then_inc(rows_spread, 16)

            def body(b, first, last):
                if not last:
                    sp.wait_ge(ctx_lo_done, b * CHUNKS + CHUNKS)
                    sp.wait_ge(ctxT_ready, b * CHUNKS + CHUNKS)
                    load_ctx(sp, b + 1)
                for g in range(NG):
                    spread_reciprocals(b, g, first)
            batches(sp, body)

            sp.wait_ge(result_ready, B // 2)
            sp.dma_start(out[0:B // 2].rearrange("b q d -> q b d"), z[:, 0:B // 2, :]).then_inc(stored, 16)
            sp.wait_ge(result_ready, B)
            sp.dma_start(out[B // 2:B].rearrange("b q d -> q b d"), z[:, B // 2:B, :]).then_inc(stored, 16)
            sp.wait_ge(stored, 32)

        @block.gpsimd
        def _(pool):
            pool.memset(ident[:, :], 0.0).then_inc(ident_zeroed, 1)
            pool.wait_ge(ident_zeroed, 1)
            pool.affine_select(out=ident[:, :], in_=ident[:, :], compare_op=ALU.not_equal, fill=1.0, base=0,
                               pattern=[[-1, P]], channel_multiplier=1).then_inc(ident_ready, 1)
            pool.memset(one[:, :, :], 1.0).then_inc(filler_set, 1)
            for part in (q_hi, q_lo):
                pool.memset(part[:, ROWS:TILES * P].bitcast(F32), 0.0).then_inc(filler_set, 1)

            def body(b, first, last):
                if first:
                    pool.wait_ge(filler_set, 1)
                pool.wait_ge(ctx_loaded, b * 32 + 32)
                for c in range(CHUNKS):
                    part = (slice(0, keys_on(c)), slice(CS * c, CS * c + CS))
                    if not first:
                        pool.wait_ge(pv_done, b * NG * CHUNKS + (c + 1 - CHUNKS))
                    pool.tensor_tensor(ctx_hi[part], ctx_in[part],
                                       one[0:keys_on(c), :, :].broadcast_to([keys_on(c), CS, P]), ALU.mult).then_inc(ctx_hi_done, 1)
                    pool.wait_ge(ctx_hi_done, b * CHUNKS + c + 1)
                    pool.tensor_tensor(ctx_lo[part], ctx_in[part], ctx_hi[part].bitcast(F32), ALU.subtract)\
                        .then_inc(ctx_lo_done, 1)
                if first:
                    pool.wait_ge(x_loaded, 16)
                    pool.wait_ge(rows_loaded, 48)
                    pool.tensor_tensor(x_res[:, :, :], x_in[:, :, :],
                                       rows_in[:, 0:1, :].broadcast_to([Q, B, P]), ALU.add).then_inc(x_res_ready, 1)
            batches(pool, body)

        @block.tensor
        def _(pe):
            def scores(dst, parity, t, c):
                lhs = slice(P * t, P * t + P)
                keys = slice(START[c], START[c] + WIDTH[c])
                o = dst[:, 0:WIDTH[c]]
                pe.matmul(o, q_hi[:, lhs], ctxT_hi[:, parity, keys], start=True, stop=False)
                pe.matmul(o, q_hi[:, lhs], ctxT_lo[:, parity, keys], start=False, stop=False)
                pe.matmul(o, q_lo[:, lhs], ctxT_hi[:, parity, keys], start=False, stop=True).then_inc(scores_ready, 1)

            def transpose_ctx(dst, c):
                n = keys_on(c)
                for i in range(CS):
                    last = pe.transpose(dst[:, n * i:n * i + n], ctx_in[0:n, CS * c + i, :], ident[0:n, 0:n])
                last.then_inc(ctxT_ready, 1)

            def project_queries(dst, b, n):
                for i in range(QG):
                    last = pe.matmul(dst[:, Q * i:Q * i + Q], A[:, QG * n + i, :], xT[:, bass.ds(b * Q, Q)],
                                     start=True, stop=True)
                last.then_inc(q_ready, 1)

            pe.wait_ge(ident_ready, 1)
            for n, e in enumerate(early):
                dst = ring[early_bank[e]]
                if n >= RING:
                    pe.wait_ge(*early_read_out(early[n - RING]))
                kind = e[0]
                if kind == "xT":
                    pe.wait_ge(x_loaded, 16)
                    for i in range(B // 2):
                        last = pe.transpose(dst[:, Q * i:Q * i + Q], x_in[:, B // 2 * e[1] + i, :], ident[0:Q, 0:Q])
                elif kind in ("wqT", "wkT", "wvT"):
                    source, loaded = {"wqT": (w_in, wq_loaded), "wkT": (wk_in, wk_loaded), "wvT": (w_in, wv_loaded)}[kind]
                    pe.wait_ge(loaded, 16)
                    for i in range(4):
                        pair = 4 * e[1] + i
                        last = pe.transpose(dst[:, P * i:P * i + P], source[:, P * pair:P * pair + P], ident[:, :])
                elif kind in ("A", "M"):
                    pe.wait_ge(early_copied, copied(("wkT", 1) if kind == "A" else ("wvT", 1)))
                    if kind == "M":
                        pe.wait_ge(fc_loaded, 16)
                    right = wkT if kind == "A" else fc_in
                    for i in range(4):
                        h = 8 * (e[1] // 2) + 2 * i + e[1] % 2
                        half = slice(KD * (h % 2), KD * (h % 2) + KD)
                        last = pe.matmul(dst[:, P * i:P * i + P], wT[half, h // 2, :], right[half, h // 2, :],
                                         start=True, stop=True)
                elif kind == "ctxT":
                    pe.wait_ge(ctx_loaded, 32)
                    transpose_ctx(dst, e[1])
                elif kind == "q":
                    pe.wait_ge(early_copied, copied(("A", 2 * (e[1] // 2) + 1)))
                    project_queries(dst, 0, e[1])
                else:
                    pe.wait_ge(ctxT_lo_done, e[2] + 1)
                    pe.wait_ge(q_lo_done, 1)
                    pe.wait_ge(filler_set, 3)
                    scores(dst, 0, 0, e[2])
                if kind not in ("ctxT", "q", "s"):
                    last.then_inc(early_filled, 1)

            def body(b, first, last):
                def next_scores(t, c):
                    e = ("s", t + 1, c)
                    dst = ring[bank_of[e]]
                    pe.wait_ge(*bank_free(e, b, first, last))
                    ahead = t == TILES - 1
                    tile, at = (0, b + 1) if ahead else (t + 1, b)
                    if c == 0:
                        pe.wait_ge(q_lo_done, at * 4 + q_block_of(tile) + 1)
                    if ahead:
                        pe.wait_ge(ctxT_lo_done, at * CHUNKS + c + 1)
                    scores(dst, at % 2, tile, c)

                def transpose_weights(t, c):
                    k = CHUNKS * t + c
                    n = keys_on(c)
                    dst = tbank[k % TBANKS]
                    pe.wait_ge(exp_done, b * NC + k + 1)
                    if k >= TBANKS or not first:
                        pe.wait_ge(wt_lo_done, b * NC + (k - TBANKS + 1 if k >= TBANKS else -((NC - 1 - k) % TBANKS)))
                    for i in range(CS):
                        at = START[c] + n * i
                        done = pe.transpose(dst[0:n, i, :], weights[:, t % 2, at:at + n], ident[:, :])
                    done.then_inc(wt_ready, 1)

                def side(t, kind, n):
                    dst = ring[bank_of[kind, t, n]]
                    pe.wait_ge(*bank_free((kind, t, n), b, first, last))
                    if kind == "q":
                        project_queries(dst, b + 1, n)
                    elif kind == "ctxT":
                        pe.wait_ge(ctx_loaded, b * 32 + 64)
                        transpose_ctx(dst, n)
                    else:
                        pe.wait_ge(attended_done, b * NG)
                        project_out(dst, 0, HEADS)

                def context_product(t):
                    g = group_of(t)
                    c = t - GROUPS[g].start
                    if c >= CHUNKS or (first and g == 0):
                        return
                    pending = g - 1 if g else NG - 1
                    group_number = b * NG + g - 1
                    ahead = b * NC + CHUNKS * (GROUPS[g].start - 1) + c + 1
                    pe.wait_ge(wt_lo_done, ahead)
                    if g == 1:
                        pe.wait_ge(ctx_lo_done, b * CHUNKS + c + 1)
                    if c == 0 and not (first and g == 1):
                        pe.wait_ge(attended_done, group_number)
                    product_chunk(pending, c)

                for t in range(TILES):
                    ahead = not (last and t == TILES - 1)
                    if t == TILES - 1:
                        for kind, n in side_work(t, first, last):
                            side(t, kind, n)
                    for c in range(CHUNKS):
                        if ahead:
                            next_scores(t, c)
                        transpose_weights(t, c)
                    if t < TILES - 1:
                        for kind, n in side_work(t, first, last):
                            side(t, kind, n)
                    context_product(t)

            def product_chunk(g, c):
                n = keys_on(c)
                w = group_rows(g)
                for s in range(CS * c, CS * c + CS):
                    hi, lo = wt_hi[g % 2][0:n, s, 0:w], wt_lo[g % 2][0:n, s, 0:w]
                    pe.matmul(pv[:, 0:w], ctx_hi[0:n, s, :], hi, start=(s == 0), stop=False)
                    pe.matmul(pv[:, 0:w], ctx_lo[0:n, s, :], hi, start=False, stop=False)
                    done = pe.matmul(pv[:, 0:w], ctx_hi[0:n, s, :], lo, start=False, stop=(s == SLOTS - 1))
                done.then_inc(pv_done, 1)

            def project_out(dst, h0, h1):
                for h in range(h0, h1):
                    done = pe.matmul(dst[0:Q, 0:V], attended[:, Q * h:Q * h + Q], M[:, h, :],
                                     start=(h == 0), stop=(h == HEADS - 1))
                if h1 == HEADS:
                    done.then_inc(proj_ready, 1)

            batches(pe, body)

            for c in range(CHUNKS):
                pe.wait_ge(wt_lo_done, B * NC - CHUNKS + c + 1)
                if c == 0:
                    pe.wait_ge(attended_done, B * NG - 1)
                product_chunk(NG - 1, c)
            pe.wait_ge(exp_done, B * NC)
            pe.wait_ge(y_ready, B - 1)
            early_heads = P * GROUPS[-1].start // Q
            project_out(ring[1], 0, early_heads)
            pe.wait_ge(attended_done, B * NG)
            project_out(ring[1], early_heads, HEADS)

        @block.scalar
        def _(act):
            act.dma_start(wk_in[:, :], w_k).then_inc(wk_loaded, 16)
            for n, row in enumerate((fc_b, ln_g, ln_b)):
                act.dma_start(rows_in[:, n, :], row.rearrange("(a d) -> a d", a=1).broadcast_to([Q, P]))\
                  .then_inc(rows_loaded, 16)

            def exp_chunk(src, b, t, c):
                act.activation(weights[:, t % 2, START[c]:START[c] + WIDTH[c]], src[:, 0:WIDTH[c]], ACT.Exp,
                               bias=neg_max[:, t:t + 1], accum_out=row_sum[:, t, c:c + 1]).then_inc(exp_done, 1)

            def q_high(src, b, n):
                act.wait_ge(q_ready, b * 4 + n + 1)
                act.activation(q_hi[:, QB * n:QB * n + QB], src[:, 0:QB], ACT.Copy).then_inc(q_hi_done, 1)

            def ctxT_high(src, b, c):
                act.wait_ge(ctxT_ready, b * CHUNKS + c + 1)
                act.activation(ctxT_hi[:, b % 2, START[c]:START[c] + WIDTH[c]], src[:, 0:WIDTH[c]], ACT.Copy)\
                   .then_inc(ctxT_hi_done, 1)

            for n, e in enumerate(early):
                src = ring[early_bank[e]]
                if e[0] == "q":
                    q_high(src, 0, e[1])
                elif e[0] == "ctxT":
                    ctxT_high(src, 0, e[1])
                elif e[0] == "s":
                    if e[2] == 0:
                        act.wait_ge(max_ready, 1)
                    exp_chunk(src, 0, 0, e[2])

            def side(b, t, first, last):
                for kind, n in side_work(t, first, last):
                    src = ring[bank_of[kind, t, n]]
                    if kind == "q":
                        q_high(src, b + 1, n)
                    elif kind == "ctxT":
                        ctxT_high(src, b + 1, n)

            def body(b, first, last):
                for t in range(TILES):
                    g = group_of(t)
                    r = rows(t)
                    at = P * (t - GROUPS[g].start)
                    if t == TILES - 1:
                        side(b, t, first, last)
                    for c in range(CHUNKS):
                        k = CHUNKS * t + c
                        n = keys_on(c)
                        act.wait_ge(wt_ready, b * NC + k + 1)
                        if not (first and g < 2):
                            act.wait_ge(pv_done, (b * NG + (g - 2)) * CHUNKS + c + 1)
                        act.activation(wt_hi[g % 2][0:n, CS * c:CS * c + CS, at:at + r],
                                       tbank[k % TBANKS][0:n, :, 0:r], ACT.Copy).then_inc(wt_hi_done, 1)
                    if not (last and t == TILES - 1):
                        tile, bb = (0, b + 1) if t == TILES - 1 else (t + 1, b)
                        act.wait_ge(max_ready, bb * TILES + tile + 1)
                        for c in range(CHUNKS):
                            e = ("s", t + 1, c)
                            src = ring[bank_of[e]]
                            if tile == 0:
                                act.wait_ge(wt_ready, bb * NC + (c + 1 - CHUNKS))
                            exp_chunk(src, bb, tile, c)
                    if t < TILES - 1:
                        side(b, t, first, last)
            batches(act, body)
            act.activation(unused[:, :], one[0:Q, 0, :], ACT.Sqrt)
            act.wait_ge(var_ready, B)
            act.activation(std[:, :], var[:, :], ACT.Sqrt).then_inc(std_ready, 1)

        @block.vector
        def _(dve):
            def chunk_maximum(src, b, t, c):
                dve.wait_ge(scores_ready, b * NC + (CHUNKS * t + c + 1))
                dve.tensor_reduce(mx[:, t, c:c + 1], src[:, 0:WIDTH[c]], AX.X, ALU.max).then_inc(chunk_max, 1)

            def tile_maximum(b, t):
                dve.wait_ge(chunk_max, b * NC + CHUNKS * (t + 1))
                dve.tensor_reduce(neg_max[:, t:t + 1], mx[:, t, :], AX.X, ALU.max, negate=True)\
                   .then_inc(max_ready, 1)

            def q_low(src, b, n):
                part = slice(QB * n, QB * n + QB)
                dve.wait_ge(q_hi_done, b * 4 + n + 1)
                dve.tensor_tensor(q_lo[:, part], src[:, 0:QB], q_hi[:, part].bitcast(F32), ALU.subtract)\
                   .then_inc(q_lo_done, 1)

            def ctxT_low(src, b, c):
                part = slice(START[c], START[c] + WIDTH[c])
                dve.wait_ge(ctxT_hi_done, b * CHUNKS + c + 1)
                dve.tensor_tensor(ctxT_lo[:, b % 2, part], src[:, 0:WIDTH[c]],
                                  ctxT_hi[:, b % 2, part].bitcast(F32), ALU.subtract).then_inc(ctxT_lo_done, 1)

            def attend(b, g):
                w = group_rows(g)
                at = P * GROUPS[g].start
                dve.wait_ge(pv_done, (b * NG + g) * CHUNKS + CHUNKS)
                dve.wait_ge(rows_spread, b * NG * 16 + (g + 1) * 16)
                n = len(GROUPS[g])
                by_tile = recip_rows[:, 0:P * n].rearrange("p (r t) -> p t r", t=n)
                full = w // P
                done = dve.tensor_tensor(attended[:, at:at + P * full].rearrange("p (t r) -> p t r", t=full),
                                         pv[:, 0:P * full].rearrange("p (t r) -> p t r", t=full),
                                         by_tile[:, 0:full, :], ALU.mult)
                if w > P * full:
                    done = dve.tensor_tensor(attended[:, at + P * full:at + w], pv[:, P * full:w],
                                             by_tile[:, full, 0:w - P * full], ALU.mult)
                done.then_inc(attended_done, 1)

            def normalise(src, b, count):
                dve.wait_ge(proj_ready, count)
                dve.scalar_tensor_tensor(y[:, :], src[0:Q, 0:V], 1.0, x_res[:, b, :], ALU.mult, ALU.add,
                                         accum_out=y_sum[:, :]).then_inc(y_ready, 1)
                dve.wait_ge(y_ready, count)
                dve.tensor_scalar(y_mean[:, :], y_sum[:, :], 1.0 / V, None, ALU.mult).then_inc(mean_ready, 1)
                dve.wait_ge(mean_ready, count)
                dve.tensor_scalar(centred[:, :], y[:, :], y_mean[:, 0:1], None, ALU.subtract).then_inc(centred_ready, 1)
                dve.wait_ge(centred_ready, count)
                dve.scalar_tensor_tensor(y[:, :], centred[:, :], 1.0, centred[:, :], ALU.mult, ALU.mult,
                                         accum_out=squares[:, :]).then_inc(squares_ready, 1)
                dve.tensor_tensor(z[:, b, :], centred[:, :], rows_in[:, 1, :], ALU.mult).then_inc(z_ready, 1)
                dve.wait_ge(squares_ready, count)
                dve.tensor_scalar(var[:, bass.ds(b, 1)], squares[:, :], 1.0 / V, LN_EPS, ALU.mult, ALU.add)\
                   .then_inc(var_ready, 1)

            for n, e in enumerate(early):
                src = ring[early_bank[e]]
                if e[0] == "q":
                    q_low(src, 0, e[1])
                elif e[0] == "ctxT":
                    ctxT_low(src, 0, e[1])
                elif e[0] == "s":
                    chunk_maximum(src, 0, 0, e[2])
                    if e[2] == CHUNKS - 1:
                        tile_maximum(0, 0)
                else:
                    dve.wait_ge(early_filled, copied(e))
                    if e[0] == "xT":
                        w = B // 2 * Q
                        copy = dve.tensor_copy(xT[:, w * e[1]:w * e[1] + w], src[:, 0:w])
                    elif e[0] in ("A", "M"):
                        dst = A if e[0] == "A" else M
                        h = 8 * (e[1] // 2) + e[1] % 2
                        scale = 1.0 / TEMPERATURE if e[0] == "A" else 1.0
                        copy = dve.tensor_scalar(dst[:, h:h + 7:2, :], src[:, :].rearrange("p (h d) -> p h d", h=4),
                                                 scale, None, ALU.mult)
                    else:
                        dst = {"wqT": wT, "wkT": wkT, "wvT": wT}[e[0]]
                        copy = dve.tensor_copy(dst[:, 4 * e[1]:4 * e[1] + 4, :],
                                               src[:, :].rearrange("p (h d) -> p h d", h=4))
                    copy.then_inc(early_copied, 1)

            def side(b, t, first, last):
                for step in [t - 1, t] if t == TILES - 1 else [t - 1] if t else []:
                    for kind, n in side_work(step, first, last):
                        src = ring[bank_of[kind, step, n]]
                        if kind == "q":
                            q_low(src, b + 1, n)
                        elif kind == "ctxT":
                            ctxT_low(src, b + 1, n)
                        else:
                            normalise(src, b - 1, b)

            def body(b, first, last):
                for t in range(TILES):
                    g = group_of(t)
                    r = rows(t)
                    at = P * (t - GROUPS[g].start)
                    if t == GROUPS[g].start + CHUNKS and g == NG - 1:
                        attend(b, g - 1)
                    elif t == GROUPS[g].start and g > 1:
                        attend(b, g - 2)
                    elif t == GROUPS[1].start and not first:
                        attend(b - 1, NG - 1)
                    for c in range(CHUNKS):
                        if not (last and t == TILES - 1):
                            tile, bb = (0, b + 1) if t == TILES - 1 else (t + 1, b)
                            src = ring[bank_of["s", t + 1, c]]
                            chunk_maximum(src, bb, tile, c)
                            if c == CHUNKS - 1:
                                tile_maximum(bb, tile)
                        k = CHUNKS * t + c
                        n = keys_on(c)
                        hi = wt_hi[g % 2][0:n, CS * c:CS * c + CS, at:at + r]
                        dve.wait_ge(wt_hi_done, b * NC + k + 1)
                        dve.tensor_tensor(wt_lo[g % 2][0:n, CS * c:CS * c + CS, at:at + r],
                                          tbank[k % TBANKS][0:n, :, 0:r], hi.bitcast(F32), ALU.subtract)\
                           .then_inc(wt_lo_done, 1)
                        if c == 0:
                            side(b, t, first, last)
                    if t == GROUPS[g].stop - 1:
                        tiles = slice(GROUPS[g].start, GROUPS[g].stop)
                        dve.wait_ge(exp_done, b * NC + CHUNKS * GROUPS[g].stop)
                        dve.tensor_reduce(total[:, tiles], row_sum[:, tiles, :], AX.X, ALU.add).then_inc(total_ready, 1)
                        dve.wait_ge(total_ready, b * NG + g + 1)
                        dve.reciprocal(recip[:, tiles], total[:, tiles]).then_inc(recip_ready, 1)
                if first:
                    dve.wait_ge(x_res_ready, 1)
            batches(dve, body)

            attend(B - 1, NG - 1)
            normalise(ring[1], B - 1, B)
            dve.wait_ge(z_ready, B)
            dve.wait_ge(std_ready, 1)
            dve.reciprocal(rstd[:, :], std[:, :]).then_inc(rstd_ready, 1)
            dve.wait_ge(rstd_ready, 1)
            for b in range(B):
                dve.scalar_tensor_tensor(z[:, b, :], z[:, b, :], rstd[:, b:b + 1], rows_in[:, 2, :],
                                         ALU.mult, ALU.add).then_inc(result_ready, 1)


_INS = ["x", "ctx_1024", "L0_xattn_W_qs", "L0_xattn_W_ks", "L0_xattn_W_vs", "L0_xattn_fc_w", "L0_xattn_fc_b",
        "L0_xattn_ln_g", "L0_xattn_ln_b"]


def kernel(**inputs):
    import numpy as _np
    import concourse.bacc as _bacc
    from concourse import mybir as _mybir
    from concourse.bass_utils import run_bass_kernel_spmd as _run

    nc = _bacc.Bacc("TRN2", target_bir_lowering=False, num_devices=1)
    arrays, args = {}, []
    for name in _INS:
        a = _np.ascontiguousarray(inputs[name])
        arrays[f"in_{name}_dram"] = a
        args.append(nc.dram_tensor(f"in_{name}_dram", a.shape, _mybir.dt.from_np(a.dtype), kind="ExternalInput").ap())
    shape = inputs["x"].shape
    args.append(nc.dram_tensor("out_0_dram", shape, _mybir.dt.float32, kind="ExternalOutput").ap())
    cross_attention(nc, *args)
    r = _run(nc, [arrays], core_ids=[0])
    return r.results[0]["out_0_dram"]
```

```python
from contextlib import ExitStack

import concourse.bass as bass
from concourse import mybir

F32 = mybir.dt.float32
F32R = mybir.dt.float32r
ALU = mybir.AluOpType
ACT = mybir.ActivationFunctionType
AX = mybir.AxisListType

P = 128
HEADS = 16
WARM_UP = 6
WARM = {}
KD = 64
TEMPERATURE = float(KD) ** 0.5
LN_EPS = 1e-5

SLOTS = 12
CHUNKS = 3
CS = SLOTS // CHUNKS
QG = 4
RING = 5
TBANKS = 2
GROUPS = [range(0, 3), range(3, 6), range(6, 9), range(9, 13)]
NG = len(GROUPS)
PRODUCT_SLOTS = [4, 4, 4, 5, 3, 4, 4, 4, 4, 3, 3, 2, 4]

SIDE = {2: [("q", 0)], 4: [("proj", 0)], 5: [("ctxT", 0)], 6: [("q", 1)], 7: [("ctxT", 1)], 8: [("q", 2)],
        9: [("ctxT", 2)], 11: [("q", 3)]}
NEXT = ("q", "ctxT")
PREV = ("proj",)


def cross_attention(nc, x, ctx, w_q, w_k, w_v, fc_w, fc_b, ln_g, ln_b, out):
    B, Q, D = x.shape
    K = ctx.shape[1]
    V = fc_w.shape[1]
    ROWS = HEADS * Q
    TILES = -(-ROWS // P)
    PAIRS = HEADS * KD // P
    WHALF = HEADS * KD // 2
    FULL, REST = divmod(K, SLOTS)
    assert D == P and V == P and Q <= P and REST == CS and TILES == GROUPS[-1].stop

    def keys_on(c):
        return FULL + 1 if c == 0 else FULL

    WIDTH = [CS * keys_on(c) for c in range(CHUNKS)]
    START = [sum(WIDTH[:c]) for c in range(CHUNKS)]
    assert sum(WIDTH) == K and max(WIDTH) <= 512

    def rows(t):
        return min(P, ROWS - P * t)

    def group_of(t):
        return next(g for g in range(NG) if t in GROUPS[g])

    def group_rows(g):
        return sum(rows(t) for t in GROUPS[g])

    NC = CHUNKS * TILES
    QBLOCKS = HEADS // QG
    QB = QG * Q

    def q_block_of(t):
        return (P * t + rows(t) - 1) // QB

    def step_entries(t):
        scores = [("s", t + 1, c) for c in range(CHUNKS)]
        side = [(kind, t, n) for kind, n in SIDE.get(t, [])]
        return side + scores if t == TILES - 1 else scores + side

    order = [e for t in range(TILES) for e in step_entries(t)]
    short = -len(order) % RING
    rounds = [RING - 1] * short + [RING] * ((len(order) - short * (RING - 1)) // RING)
    bank_of = dict(zip(order, [bank for r in rounds for bank in range(r)], strict=True))
    early = ([("wqT", 0), ("wkT", 0), ("xT", 0), ("A", 0), ("A", 1)] + [("ctxT", c) for c in range(CHUNKS)]
             + [("q", 0), ("wqT", 1), ("wkT", 1)] + [("s", 0, c) for c in range(CHUNKS)]
             + [("A", 2), ("A", 3), ("q", 1)])
    LATE = {(0, 0): [("q", 2)], (0, 1): [("wvT", 0)], (0, 2): [("wvT", 1)],
            (1, 0): [("q", 3)], (1, 1): [("M", 0)], (1, 2): [("M", 1)],
            (2, 0): [("M", 2)], (2, 1): [("M", 3)], (2, 2): [("xT", 1)]}
    late = [e for key in LATE for e in LATE[key]]
    LATE_STEPS = GROUPS[0].stop
    BY_ACT = [("wkT", 0), ("A", 1), ("wkT", 1), ("A", 3), ("wvT", 0), ("M", 0), ("M", 2)]
    plain = [e for e in early + late if e[0] not in ("s", "q", "ctxT")]

    NEAR = 5
    PV_BANK, T_BANK = RING, RING + 1
    first_order, start_bank = list(early), {}
    for t in range(LATE_STEPS):
        for c in range(CHUNKS):
            first_order += [("s", t + 1, c), ("t", t, c)] + LATE[t, c]
        first_order += [e for e in step_entries(t)[CHUNKS:] if e[0] not in PREV]
    rest = [e for t in range(LATE_STEPS, TILES) for e in step_entries(t) if e[0] not in PREV]
    next_use = {bank: min(len(first_order) + n for n, e in enumerate(rest) if bank_of[e] == bank) for bank in range(RING)}
    next_use |= {PV_BANK: len(first_order)} | {T_BANK + i: len(first_order) for i in range(TBANKS)}
    for n in reversed(range(len(first_order))):
        e = first_order[n]
        choice = ([T_BANK + (CHUNKS * e[1] + e[2]) % TBANKS] if e[0] == "t" else
                  [bank for bank in next_use if n >= len(early) and bank < T_BANK or n < len(early) and bank != PV_BANK])
        near = [bank for bank in choice if next_use[bank] - n >= NEAR]
        if n >= len(early) and e[0] != "s" and near:
            start_bank[e] = min(near, key=lambda bank: next_use[bank])
        else:
            start_bank[e] = max(choice, key=lambda bank: next_use[bank])
        next_use[start_bank[e]] = n
    first_order += rest
    PRODUCT, taken = {}, 0
    for t, count in enumerate(PRODUCT_SLOTS):
        PRODUCT[t] = range(taken % SLOTS, taken % SLOTS + count)
        taken += count
    assert all(sum(len(PRODUCT[t]) for t in group) == SLOTS for group in GROUPS)
    def filled(e):
        return plain.index(e) + 1

    with ExitStack() as stack:
        def sb(name, shape, dt=F32):
            return stack.enter_context(nc.sbuf_tensor(name, shape, dt))

        def sem(name):
            return stack.enter_context(nc.semaphore(name))

        ident = sb("ident", [P, P])
        recip_line = nc.dram_tensor("recip_line", [NG, 512], F32, kind="Internal").ap()
        zeros = sb("zeros", [P, P])
        one = sb("one", [P, 1, 1])
        ctx_in = sb("ctx_in", [P, SLOTS, P])
        ctx_hi = sb("ctx_hi", [P, SLOTS, P], F32R)
        ctx_lo = sb("ctx_lo", [P, SLOTS, P], F32R)
        ctxT_hi = sb("ctxT_hi", [P, 2, K], F32R)
        ctxT_lo = sb("ctxT_lo", [P, 2, K], F32R)
        q_hi = sb("q_hi", [P, TILES * P], F32R)
        q_lo = sb("q_lo", [P, TILES * P], F32R)
        weights = sb("weights", [P, 2, K])
        wt_hi = [sb(f"wt_hi{i}", [P, SLOTS, group_rows(2 + i)], F32R) for i in range(2)]
        wt_lo = [sb(f"wt_lo{i}", [P, SLOTS, group_rows(2 + i)], F32R) for i in range(2)]
        mx = sb("mx", [P, TILES, CHUNKS])
        neg_max = sb("neg_max", [P, TILES])
        row_sum = sb("row_sum", [P, TILES, CHUNKS])
        total = sb("total", [P, TILES])
        recip = sb("recip", [P, TILES])
        recip_rows = sb("recip_rows", [P, P * len(GROUPS[-1])])
        attended = sb("attended", [P, ROWS])
        A = sb("A", [P, HEADS, P])
        M = sb("M", [P, HEADS, P])
        xT = sb("xT", [P, B * Q])
        x_in = sb("x_in", [Q, B, P])
        x_res = sb("x_res", [Q, B, P])
        w_in = sb("w_in", [P, HEADS * KD])
        wk_in = sb("wk_in", [P, HEADS * KD])
        wT = sb("wT", [P, PAIRS, P])
        wkT = sb("wkT", [P, PAIRS, P])
        fc_in = sb("fc_in", [P, PAIRS, P])
        rows_in = sb("rows_in", [Q, 3, P])
        y = sb("y", [Q, P])
        y_sum, neg_mean, squares = sb("y_sum", [Q, 1]), sb("neg_mean", [Q, 1]), sb("squares", [Q, 1])
        squared = sb("squared", [Q, P])
        z = sb("z", [Q, B, P])
        var = sb("var", [Q, B])
        std = sb("std", [Q, B])
        rstd = sb("rstd", [Q, B])

        ring = [stack.enter_context(nc.psum_tensor(f"ring{i}", [P, 512], F32)) for i in range(RING)]
        tbank = [stack.enter_context(nc.psum_tensor(f"tbank{i}", [P, CS, P], F32)) for i in range(TBANKS)]
        pv = stack.enter_context(nc.psum_tensor("pv", [P, 512], F32))
        banks = ring + [pv] + [bank[:, :, :].rearrange("p s r -> p (s r)") for bank in tbank]

        ident_zeroed, ident_ready = sem("ident_zeroed"), sem("ident_ready")
        filler_set = sem("filler_set")
        x_loaded, wv_loaded = sem("x_loaded"), sem("wv_loaded")
        wq_loaded = [sem(f"wq_loaded{i}") for i in range(2)]
        wk_loaded = [sem(f"wk_loaded{i}") for i in range(2)]
        fc_loaded, rows_loaded, ctx_loaded = sem("fc_loaded"), sem("rows_loaded"), sem("ctx_loaded")
        zeros_set = sem("zeros_set")
        start_filled = sem("start_filled")
        start_copied, start_copied_act = sem("start_copied"), sem("start_copied_act")
        x_res_ready = sem("x_res_ready")
        scores_ready = sem("scores_ready")
        chunk_max = sem("chunk_max")
        max_ready = sem("max_ready")
        exp_done = sem("exp_done")
        wt_ready = sem("wt_ready")
        wt_hi_done = sem("wt_hi_done")
        wt_lo_done = sem("wt_lo_done")
        pv_done = sem("pv_done")
        total_ready = sem("total_ready")
        recip_ready = sem("recip_ready")
        recip_stored = sem("recip_stored")
        rows_spread = sem("rows_spread")
        attended_done = sem("attended_done")
        q_ready, q_hi_done, q_lo_done = sem("q_ready"), sem("q_hi_done"), sem("q_lo_done")
        ctxT_ready, ctxT_hi_done, ctxT_lo_done = sem("ctxT_ready"), sem("ctxT_hi_done"), sem("ctxT_lo_done")
        ctx_hi_done, ctx_lo_done = sem("ctx_hi_done"), sem("ctx_lo_done")
        proj_ready = sem("proj_ready")
        y_ready, mean_ready = sem("y_ready"), sem("mean_ready")
        squares_ready, z_ready = sem("squares_ready"), sem("z_ready")
        var_ready, std_ready, rstd_ready, result_ready, stored = sem("var_ready"), sem("std_ready"), sem("rstd_ready"), sem("result_ready"), sem("stored")

        def batches(eng, body):
            body(0, True, False)
            with eng.Fori(1, B - 1) as b:
                body(b, False, False)
            body(B - 1, False, True)

        def in_batch(kind, first, last):
            return not (first and kind in PREV) and not (last and kind in NEXT)

        def side_work(t, first, last):
            return [(kind, n) for kind, n in SIDE.get(t, []) if in_batch(kind, first, last)]

        def there(e, first, last):
            if e[0] == "s":
                return not (last and e[1] == TILES)
            return in_batch(e[0], first, last)

        def read_out(e, b):
            kind, t, n = e
            if kind == "s":
                return exp_done, b * NC + (CHUNKS * t + n + 1)
            if kind == "q":
                return q_lo_done, b * QBLOCKS + (QBLOCKS + n + 1)
            if kind == "ctxT":
                return ctxT_lo_done, b * CHUNKS + (CHUNKS + n + 1)
            return y_ready, b

        def copied(e):
            by_act = e in BY_ACT
            mine = [f for f in plain if (f in BY_ACT) == by_act]
            return (start_copied_act if by_act else start_copied), mine.index(e) + 1

        def start_read_out(e):
            if e[0] in ("s", "q", "ctxT"):
                n = CHUNKS * e[1] + e[2] if e[0] == "s" else e[1]
                return {"s": exp_done, "q": q_lo_done, "ctxT": ctxT_lo_done}[e[0]], n + 1
            return copied(e)

        def bank(e, first):
            return banks[start_bank.get(e, bank_of.get(e)) if first else bank_of[e]]

        def bank_free(e, b, first, last):
            if first:
                where = start_bank.get(e, bank_of.get(e))
                before = [f for f in first_order[:first_order.index(e)]
                          if start_bank.get(f, bank_of.get(f)) == where]
                if not before:
                    return None
                f = before[-1]
                return start_read_out(f) if len(f) == 2 or f[0] == "s" else read_out(f, b)
            before = [f for f in order[:order.index(e)] if bank_of[f] == bank_of[e] and there(f, first, last)]
            if before:
                return read_out(before[-1], b)
            return read_out([f for f in order if bank_of[f] == bank_of[e]][-1], b - 1)

        def place(e):
            kind, n = e
            if kind in ("A", "M"):
                h = 8 * (n // 2) + n % 2
                return ((A, 1.0 / TEMPERATURE) if kind == "A" else (M, 1.0))[0][:, h:h + 7:2, :], 1.0 / TEMPERATURE if kind == "A" else 1.0
            return (wkT if kind == "wkT" else wT)[:, 4 * n:4 * n + 4, :], 1.0

        block = stack.enter_context(nc.Block())

        def load_ctx(sp, b):
            sp.dma_start(ctx_in[0:FULL, :, :],
                         ctx[b, 0:SLOTS * FULL, :].rearrange("(p s) d -> p s d", s=SLOTS)).then_inc(ctx_loaded, 16)
            sp.dma_start(ctx_in[FULL:FULL + 1, 0:CS, :],
                         ctx[b, SLOTS * FULL:K, :].rearrange("(p s) d -> p s d", s=CS)).then_inc(ctx_loaded, 16)

        @block.sync
        def _(sp):
            sp.dma_start(w_in[:, 0:WHALF], w_q[:, 0:WHALF]).then_inc(wq_loaded[0], 16)
            sp.dma_start(x_in[:, :, :], x.rearrange("b q d -> q b d")).then_inc(x_loaded, 16)
            sp.dma_start(w_in[:, WHALF:], w_q[:, WHALF:]).then_inc(wq_loaded[1], 16)
            sp.dma_start(fc_in[:, :, :], fc_w.rearrange("(n p) d -> p n d", p=P)).then_inc(fc_loaded, 16)
            for n, row in enumerate((fc_b, ln_g, ln_b)):
                sp.dma_start(rows_in[:, n, :], row.rearrange("(a d) -> a d", a=1).broadcast_to([Q, P]))\
                  .then_inc(rows_loaded, 16)
            sp.wait_ge(start_filled, filled(("wqT", 1)))
            sp.dma_start(w_in[:, :], w_v).then_inc(wv_loaded, 16)

            def spread_reciprocals(b, g, first):
                n = len(GROUPS[g])
                sp.wait_ge(recip_ready, b * NG + g + 1)
                sp.dma_start(recip_line[g, 0:P * n].rearrange("(p t) -> p t", t=n),
                             recip[:, GROUPS[g].start:GROUPS[g].stop]).then_inc(recip_stored, 16)
                sp.wait_ge(recip_stored, b * 16 * NG + 16 * (g + 1))
                if not (first and g == 0):
                    sp.wait_ge(attended_done, b * NG + g)
                sp.dma_start(recip_rows[:, 0:P * n], recip_line[g:g + 1, 0:P * n].broadcast_to([P, P * n]))\
                  .then_inc(rows_spread, 16)

            def body(b, first, last):
                if not last:
                    sp.wait_ge(ctx_lo_done, b * CHUNKS + CHUNKS)
                    sp.wait_ge(ctxT_ready, b * CHUNKS + CHUNKS)
                    load_ctx(sp, b + 1)
                for g in range(NG):
                    spread_reciprocals(b, g, first)
            batches(sp, body)

            sp.wait_ge(result_ready, B - 1)
            sp.dma_start(out[0:B - 1].rearrange("b q d -> q b d"), z[:, 0:B - 1, :]).then_inc(stored, 16)
            sp.wait_ge(result_ready, B)
            sp.dma_start(out[B - 1], z[:, B - 1, :]).then_inc(stored, 16)
            sp.wait_ge(stored, 32)

        @block.gpsimd
        def _(pool):
            pool.memset(ident[:, :], 0.0).then_inc(ident_zeroed, 1)
            pool.wait_ge(ident_zeroed, 1)
            pool.affine_select(out=ident[:, :], in_=ident[:, :], compare_op=ALU.not_equal, fill=1.0, base=0,
                               pattern=[[-1, P]], channel_multiplier=1).then_inc(ident_ready, 1)
            pool.memset(one[:, :, :], 1.0).then_inc(filler_set, 1)
            for part in (q_hi, q_lo):
                pool.memset(part[:, ROWS:TILES * P].bitcast(F32), 0.0).then_inc(filler_set, 1)

            def body(b, first, last):
                if first:
                    pool.wait_ge(filler_set, 1)
                pool.wait_ge(ctx_loaded, b * 32 + 32)
                for c in range(CHUNKS):
                    part = (slice(0, keys_on(c)), slice(CS * c, CS * c + CS))
                    if not first:
                        pool.wait_ge(pv_done, b * NG * CHUNKS + (c + 1 - CHUNKS))
                    pool.tensor_tensor(ctx_hi[part], ctx_in[part],
                                       one[0:keys_on(c), :, :].broadcast_to([keys_on(c), CS, P]), ALU.mult).then_inc(ctx_hi_done, 1)
                    pool.wait_ge(ctx_hi_done, b * CHUNKS + c + 1)
                    pool.tensor_tensor(ctx_lo[part], ctx_in[part], ctx_hi[part].bitcast(F32), ALU.subtract)\
                        .then_inc(ctx_lo_done, 1)
                if first:
                    pool.wait_ge(x_loaded, 16)
                    pool.wait_ge(rows_loaded, 48)
                    pool.tensor_tensor(x_res[:, :, :], x_in[:, :, :],
                                       rows_in[:, 0:1, :].broadcast_to([Q, B, P]), ALU.add).then_inc(x_res_ready, 1)
            batches(pool, body)

        @block.tensor
        def _(pe):
            def wait_for_bank(e, b, first, last):
                free = bank_free(e, b, first, last)
                if free:
                    pe.wait_ge(*free)

            def scores(dst, parity, t, c):
                lhs = slice(P * t, P * t + P)
                keys = slice(START[c], START[c] + WIDTH[c])
                o = dst[:, 0:WIDTH[c]]
                pe.matmul(o, q_hi[:, lhs], ctxT_hi[:, parity, keys], start=True, stop=False)
                pe.matmul(o, q_hi[:, lhs], ctxT_lo[:, parity, keys], start=False, stop=False)
                pe.matmul(o, q_lo[:, lhs], ctxT_hi[:, parity, keys], start=False, stop=True).then_inc(scores_ready, 1)

            def transpose_ctx(dst, c):
                n = keys_on(c)
                for i in range(CS):
                    last = pe.transpose(dst[:, n * i:n * i + n], ctx_in[0:n, CS * c + i, :], ident[0:n, 0:n])
                last.then_inc(ctxT_ready, 1)

            def project_queries(dst, b, n):
                for i in range(QG):
                    last = pe.matmul(dst[:, Q * i:Q * i + Q], A[:, QG * n + i, :], xT[:, bass.ds(b * Q, Q)],
                                     start=True, stop=True)
                last.then_inc(q_ready, 1)

            def transpose_w(dst, source, n):
                for i in range(4):
                    pair = 4 * n + i
                    last = pe.transpose(dst[:, P * i:P * i + P], source[:, P * pair:P * pair + P], ident[:, :])
                return last

            def merge(dst, right, n):
                for i in range(4):
                    h = 8 * (n // 2) + 2 * i + n % 2
                    half = slice(KD * (h % 2), KD * (h % 2) + KD)
                    last = pe.matmul(dst[:, P * i:P * i + P], wT[half, h // 2, :], right[half, h // 2, :],
                                     start=True, stop=True)
                return last

            def keep_warm(n):
                for _ in range(n):
                    pe.matmul(pv[:, 0:P], zeros[:, :], zeros[:, :], start=True, stop=True)

            def start(e):
                dst = banks[start_bank[e]]
                wait_for_bank(e, 0, True, False)
                kind, n = e[0], e[1]
                if kind == "xT":
                    pe.wait_ge(x_loaded, 16)
                    for i in range(B // 2):
                        done = pe.transpose(dst[:, Q * i:Q * i + Q], x_in[:, B // 2 * n + i, :], ident[0:Q, 0:Q])
                elif kind in ("wqT", "wkT", "wvT"):
                    if kind == "wvT":
                        pe.wait_ge(wv_loaded, 16)
                    else:
                        pe.wait_ge((wq_loaded if kind == "wqT" else wk_loaded)[n], 16)
                    done = transpose_w(dst, wk_in if kind == "wkT" else w_in, n)
                elif kind == "A":
                    pe.wait_ge(*copied(("wqT", n // 2)))
                    pe.wait_ge(*copied(("wkT", n // 2)))
                    done = merge(dst, wkT, n)
                elif kind == "M":
                    pe.wait_ge(fc_loaded, 16)
                    pe.wait_ge(*copied(("wvT", n // 2)))
                    done = merge(dst, fc_in, n)
                elif kind == "ctxT":
                    pe.wait_ge(ctx_loaded, 32)
                    transpose_ctx(dst, n)
                elif kind == "q":
                    pe.wait_ge(*copied(("xT", 0)))
                    pe.wait_ge(*copied(("A", 2 * (n // 2))))
                    pe.wait_ge(*copied(("A", 2 * (n // 2) + 1)))
                    project_queries(dst, 0, n)
                else:
                    pe.wait_ge(ctxT_lo_done, e[2] + 1)
                    pe.wait_ge(q_lo_done, 1)
                    pe.wait_ge(filler_set, 3)
                    scores(dst, 0, 0, e[2])
                if kind not in ("ctxT", "q", "s"):
                    done.then_inc(start_filled, 1)

            pe.wait_ge(zeros_set, 1)
            keep_warm(WARM_UP)
            pe.wait_ge(ident_ready, 1)
            for e in early:
                keep_warm(WARM.get(e, 0))
                start(e)

            def body(b, first, last):
                def next_scores(t, c):
                    e = ("s", t + 1, c)
                    dst = bank(e, first)
                    ahead = t == TILES - 1
                    tile, at = (0, b + 1) if ahead else (t + 1, b)
                    if c == 0 and (tile == 0 or q_block_of(tile) > q_block_of(tile - 1)):
                        pe.wait_ge(q_lo_done, at * QBLOCKS + q_block_of(tile) + 1)
                    if ahead:
                        pe.wait_ge(ctxT_lo_done, at * CHUNKS + c + 1)
                    wait_for_bank(e, b, first, last)
                    scores(dst, at % 2, tile, c)

                def transpose_weights(t, c):
                    k = CHUNKS * t + c
                    n = keys_on(c)
                    dst = tbank[k % TBANKS]
                    pe.wait_ge(exp_done, b * NC + k + 1)
                    if first and k < TBANKS:
                        wait_for_bank(("t", t, c), b, first, last)
                    else:
                        pe.wait_ge(wt_lo_done, b * NC + (k - TBANKS + 1 if k >= TBANKS else -((NC - 1 - k) % TBANKS)))
                    for i in range(CS):
                        at = START[c] + n * i
                        r = rows(t) if i else P
                        done = pe.transpose(dst[0:n, i, 0:r], weights[0:r, t % 2, at:at + n], ident[0:r, 0:r])
                    done.then_inc(wt_ready, 1)

                def side(t, kind, n):
                    dst = bank((kind, t, n), first)
                    wait_for_bank((kind, t, n), b, first, last)
                    if kind == "q":
                        project_queries(dst, b + 1, n)
                    elif kind == "ctxT":
                        pe.wait_ge(ctx_loaded, b * 32 + 64)
                        transpose_ctx(dst, n)
                    else:
                        pe.wait_ge(attended_done, b * NG)
                        project_out(dst, 0, HEADS)

                def context_product(t, part=None):
                    g = group_of(t)
                    if first and g == 0:
                        return
                    slots = PRODUCT[t]
                    if part is not None:
                        slots = slots[len(slots) * part // CHUNKS:len(slots) * (part + 1) // CHUNKS]
                    for s in slots:
                        c = s // CS
                        if s % CS == 0:
                            if g == 1:
                                pe.wait_ge(ctx_lo_done, b * CHUNKS + c + 1)
                            pe.wait_ge(wt_lo_done, b * NC + CHUNKS * (GROUPS[g].start - 1) + c + 1)
                        if s == 0 and first and g == 1:
                            pe.wait_ge(*start_read_out([e for e in first_order if start_bank.get(e) == PV_BANK][-1]))
                        elif s == 0:
                            pe.wait_ge(attended_done, b * NG + g - 1)
                        product(g - 1 if g else NG - 1, s)

                for t in range(TILES):
                    ahead = not (last and t == TILES - 1)
                    if t == TILES - 1:
                        for kind, n in side_work(t, first, last):
                            side(t, kind, n)
                    for c in range(CHUNKS):
                        if ahead:
                            next_scores(t, c)
                        transpose_weights(t, c)
                        if first:
                            for e in LATE.get((t, c), []):
                                start(e)
                        if not ahead:
                            context_product(t, c)
                    if t < TILES - 1:
                        for kind, n in side_work(t, first, last):
                            side(t, kind, n)
                    if ahead:
                        context_product(t)

            def product(g, s):
                n = keys_on(s // CS)
                w = group_rows(g)
                hi, lo = wt_hi[g % 2][0:n, s, 0:w], wt_lo[g % 2][0:n, s, 0:w]
                pe.matmul(pv[:, 0:w], ctx_hi[0:n, s, :], hi, start=(s == 0), stop=False)
                pe.matmul(pv[:, 0:w], ctx_lo[0:n, s, :], hi, start=False, stop=False)
                done = pe.matmul(pv[:, 0:w], ctx_hi[0:n, s, :], lo, start=False, stop=(s == SLOTS - 1))
                if s % CS == CS - 1:
                    done.then_inc(pv_done, 1)

            def project_out(dst, h0, h1):
                for h in range(h0, h1):
                    done = pe.matmul(dst[0:Q, 0:V], attended[:, Q * h:Q * h + Q], M[:, h, :],
                                     start=(h == 0), stop=(h == HEADS - 1))
                if h1 == HEADS:
                    done.then_inc(proj_ready, 1)

            batches(pe, body)

            for c in range(CHUNKS):
                pe.wait_ge(wt_lo_done, B * NC - CHUNKS + c + 1)
                if c == 0:
                    pe.wait_ge(attended_done, B * NG - 1)
                for s in range(CS * c, CS * c + CS):
                    product(NG - 1, s)
            pe.wait_ge(exp_done, B * NC)
            pe.wait_ge(y_ready, B - 1)
            early_heads = P * GROUPS[-1].start // Q
            project_out(ring[1], 0, early_heads)
            pe.wait_ge(attended_done, B * NG)
            project_out(ring[1], early_heads, HEADS)

        @block.scalar
        def _(act):
            act.dma_start(wk_in[:, 0:WHALF], w_k[:, 0:WHALF]).then_inc(wk_loaded[0], 16)
            load_ctx(act, 0)
            act.dma_start(wk_in[:, WHALF:], w_k[:, WHALF:]).then_inc(wk_loaded[1], 16)

            def exp_chunk(src, b, t, c):
                act.activation(weights[:, t % 2, START[c]:START[c] + WIDTH[c]], src[:, 0:WIDTH[c]], ACT.Exp,
                               bias=neg_max[:, t:t + 1], accum_out=row_sum[:, t, c:c + 1]).then_inc(exp_done, 1)

            def q_high(src, b, n):
                act.wait_ge(q_ready, b * 4 + n + 1)
                act.activation(q_hi[:, QB * n:QB * n + QB], src[:, 0:QB], ACT.Copy).then_inc(q_hi_done, 1)

            def ctxT_high(src, b, c):
                act.wait_ge(ctxT_ready, b * CHUNKS + c + 1)
                act.activation(ctxT_hi[:, b % 2, START[c]:START[c] + WIDTH[c]], src[:, 0:WIDTH[c]], ACT.Copy)\
                   .then_inc(ctxT_hi_done, 1)

            def start(e):
                src = banks[start_bank[e]]
                if e[0] == "q":
                    q_high(src, 0, e[1])
                elif e[0] == "ctxT":
                    ctxT_high(src, 0, e[1])
                elif e[0] == "s":
                    if e[2] == 0:
                        act.wait_ge(max_ready, 1)
                    exp_chunk(src, 0, 0, e[2])
                elif e in BY_ACT:
                    act.wait_ge(start_filled, filled(e))
                    dst, scale = place(e)
                    act.activation(dst, src[:, :].rearrange("p (h d) -> p h d", h=4), ACT.Copy, scale=scale)\
                        .then_inc(start_copied_act, 1)

            for e in early:
                start(e)

            def sum_squares(count):
                act.wait_ge(mean_ready, count)
                act.activation(squared[:, :], y[:, :], ACT.Square, bias=neg_mean[:, 0:1], accum_out=squares[:, :])\
                   .then_inc(squares_ready, 1)

            def side(b, t, first, last):
                if ("proj", 0) in side_work(t - 1, first, last):
                    sum_squares(b)
                for kind, n in side_work(t, first, last):
                    src = bank((kind, t, n), first)
                    if kind == "q":
                        q_high(src, b + 1, n)
                    elif kind == "ctxT":
                        ctxT_high(src, b + 1, n)

            def body(b, first, last):
                for t in range(TILES):
                    g = group_of(t)
                    r = rows(t)
                    at = P * (t - GROUPS[g].start)
                    if t == TILES - 1:
                        side(b, t, first, last)
                    for c in range(CHUNKS):
                        k = CHUNKS * t + c
                        n = keys_on(c)
                        if t == GROUPS[g].start and not (first and g < 2):
                            act.wait_ge(pv_done, (b * NG + (g - 2)) * CHUNKS + c + 1)
                        act.wait_ge(wt_ready, b * NC + k + 1)
                        act.activation(wt_hi[g % 2][0:n, CS * c:CS * c + CS, at:at + r],
                                       tbank[k % TBANKS][0:n, :, 0:r], ACT.Copy).then_inc(wt_hi_done, 1)
                        if first and c < CHUNKS - 1:
                            for e in LATE.get((t, c), []):
                                start(e)
                    if not (last and t == TILES - 1):
                        tile, bb = (0, b + 1) if t == TILES - 1 else (t + 1, b)
                        act.wait_ge(max_ready, bb * TILES + tile + 1)
                        for c in range(CHUNKS):
                            e = ("s", t + 1, c)
                            src = bank(e, first)
                            if tile == 0:
                                act.wait_ge(wt_ready, bb * NC + (c + 1 - CHUNKS))
                            exp_chunk(src, bb, tile, c)
                    if first:
                        for e in LATE.get((t, CHUNKS - 1), []):
                            start(e)
                    if t < TILES - 1:
                        side(b, t, first, last)
            batches(act, body)
            act.wait_ge(var_ready, B - 1)
            act.activation(std[:, 0:B - 1], var[:, 0:B - 1], ACT.Sqrt).then_inc(std_ready, 1)
            sum_squares(B)
            act.wait_ge(var_ready, B)
            act.activation(std[:, B - 1:B], var[:, B - 1:B], ACT.Sqrt).then_inc(std_ready, 1)

        @block.vector
        def _(dve):
            def chunk_maximum(src, b, t, c):
                dve.wait_ge(scores_ready, b * NC + (CHUNKS * t + c + 1))
                dve.tensor_reduce(mx[:, t, c:c + 1], src[:, 0:WIDTH[c]], AX.X, ALU.max).then_inc(chunk_max, 1)

            def tile_maximum(b, t):
                dve.wait_ge(chunk_max, b * NC + CHUNKS * (t + 1))
                dve.tensor_reduce(neg_max[:, t:t + 1], mx[:, t, :], AX.X, ALU.max, negate=True)\
                   .then_inc(max_ready, 1)

            def q_low(src, b, n):
                part = slice(QB * n, QB * n + QB)
                dve.wait_ge(q_hi_done, b * 4 + n + 1)
                dve.tensor_tensor(q_lo[:, part], src[:, 0:QB], q_hi[:, part].bitcast(F32), ALU.subtract)\
                   .then_inc(q_lo_done, 1)

            def ctxT_low(src, b, c):
                part = slice(START[c], START[c] + WIDTH[c])
                dve.wait_ge(ctxT_hi_done, b * CHUNKS + c + 1)
                dve.tensor_tensor(ctxT_lo[:, b % 2, part], src[:, 0:WIDTH[c]],
                                  ctxT_hi[:, b % 2, part].bitcast(F32), ALU.subtract).then_inc(ctxT_lo_done, 1)

            def attend(b, g):
                w = group_rows(g)
                at = P * GROUPS[g].start
                dve.wait_ge(rows_spread, b * NG * 16 + (g + 1) * 16)
                dve.wait_ge(pv_done, (b * NG + g) * CHUNKS + CHUNKS)
                n = len(GROUPS[g])
                by_tile = recip_rows[:, 0:P * n].rearrange("p (r t) -> p t r", t=n)
                full = w // P
                done = dve.tensor_tensor(attended[:, at:at + P * full].rearrange("p (t r) -> p t r", t=full),
                                         pv[:, 0:P * full].rearrange("p (t r) -> p t r", t=full),
                                         by_tile[:, 0:full, :], ALU.mult)
                if w > P * full:
                    done = dve.tensor_tensor(attended[:, at + P * full:at + w], pv[:, P * full:w],
                                             by_tile[:, full, 0:w - P * full], ALU.mult)
                done.then_inc(attended_done, 1)

            def normalise(src, b, count):
                dve.wait_ge(proj_ready, count)
                dve.scalar_tensor_tensor(y[:, :], src[0:Q, 0:V], 1.0, x_res[:, b, :], ALU.mult, ALU.add,
                                         accum_out=y_sum[:, :]).then_inc(y_ready, 1)
                dve.wait_ge(y_ready, count)
                dve.tensor_scalar(neg_mean[:, :], y_sum[:, :], -1.0 / V, None, ALU.mult).then_inc(mean_ready, 1)
                dve.wait_ge(mean_ready, count)
                dve.scalar_tensor_tensor(z[:, b, :], y[:, :], neg_mean[:, 0:1], rows_in[:, 1, :], ALU.add, ALU.mult)\
                   .then_inc(z_ready, 1)

            def variance(b, count):
                dve.wait_ge(squares_ready, count)
                dve.tensor_scalar(var[:, bass.ds(b, 1)], squares[:, :], 1.0 / V, LN_EPS, ALU.mult, ALU.add)\
                   .then_inc(var_ready, 1)

            def start(e):
                src = banks[start_bank[e]]
                if e[0] == "q":
                    q_low(src, 0, e[1])
                elif e[0] == "ctxT":
                    ctxT_low(src, 0, e[1])
                elif e[0] == "s":
                    chunk_maximum(src, 0, 0, e[2])
                    if e[2] == CHUNKS - 1:
                        tile_maximum(0, 0)
                elif e not in BY_ACT:
                    dve.wait_ge(start_filled, filled(e))
                    if e[0] == "xT":
                        w = B // 2 * Q
                        copy = dve.tensor_copy(xT[:, w * e[1]:w * e[1] + w], src[:, 0:w])
                    else:
                        dst, scale = place(e)
                        copy = dve.tensor_scalar(dst, src[:, :].rearrange("p (h d) -> p h d", h=4), scale, None,
                                                 ALU.mult)
                    copy.then_inc(start_copied, 1)

            dve.memset(zeros[:, :], 0.0).then_inc(zeros_set, 1)
            for e in early:
                start(e)

            def side(b, t, first, last):
                for step in [t - 1, t] if t == TILES - 1 else [t - 1] if t else []:
                    for kind, n in side_work(step, first, last):
                        src = bank((kind, step, n), first)
                        if kind == "q":
                            q_low(src, b + 1, n)
                        elif kind == "ctxT":
                            ctxT_low(src, b + 1, n)
                        else:
                            normalise(src, b - 1, b)

            def body(b, first, last):
                for t in range(TILES):
                    g = group_of(t)
                    r = rows(t)
                    at = P * (t - GROUPS[g].start)
                    def next_maximum(c):
                        if last and t == TILES - 1:
                            return
                        tile, bb = (0, b + 1) if t == TILES - 1 else (t + 1, b)
                        chunk_maximum(bank(("s", t + 1, c), first), bb, tile, c)
                        if c == CHUNKS - 1:
                            tile_maximum(bb, tile)

                    def low_half(c):
                        k = CHUNKS * t + c
                        n = keys_on(c)
                        hi = wt_hi[g % 2][0:n, CS * c:CS * c + CS, at:at + r]
                        dve.wait_ge(wt_hi_done, b * NC + k + 1)
                        dve.tensor_tensor(wt_lo[g % 2][0:n, CS * c:CS * c + CS, at:at + r],
                                          tbank[k % TBANKS][0:n, :, 0:r], hi.bitcast(F32), ALU.subtract)\
                           .then_inc(wt_lo_done, 1)

                    if t == GROUPS[g].start:
                        if g > 1:
                            attend(b, g - 2)
                        elif not first:
                            attend(b - 1, g + NG - 2)
                    next_maximum(0)
                    if ("proj", 0) in side_work(t - 2, first, last):
                        variance(b - 1, b)
                    low_half(0)
                    next_maximum(1)
                    if first:
                        for e in LATE.get((t, 0), []):
                            start(e)
                    if t == TILES - 1:
                        side(b, t, first, last)
                    next_maximum(2)
                    low_half(1)
                    if first:
                        for e in LATE.get((t, 1), []):
                            start(e)
                    if t < TILES - 1:
                        side(b, t, first, last)
                    low_half(2)
                    if first:
                        for e in LATE.get((t, CHUNKS - 1), []):
                            start(e)
                    if t == GROUPS[g].stop - 1:
                        tiles = slice(GROUPS[g].start, GROUPS[g].stop)
                        dve.wait_ge(exp_done, b * NC + CHUNKS * GROUPS[g].stop)
                        dve.tensor_reduce(total[:, tiles], row_sum[:, tiles, :], AX.X, ALU.add).then_inc(total_ready, 1)
                        dve.wait_ge(total_ready, b * NG + g + 1)
                        dve.reciprocal(recip[:, tiles], total[:, tiles]).then_inc(recip_ready, 1)
                if first:
                    dve.wait_ge(x_res_ready, 1)
            batches(dve, body)

            def finish(b0, b1, count):
                dve.wait_ge(std_ready, count)
                dve.reciprocal(rstd[:, b0:b1], std[:, b0:b1]).then_inc(rstd_ready, 1)
                dve.wait_ge(rstd_ready, count)
                dve.wait_ge(z_ready, b1)
                for b in range(b0, b1):
                    dve.scalar_tensor_tensor(z[:, b, :], z[:, b, :], rstd[:, b:b + 1], rows_in[:, 2, :],
                                             ALU.mult, ALU.add).then_inc(result_ready, 1)

            attend(B - 1, NG - 2)
            finish(0, B - 1, 1)
            attend(B - 1, NG - 1)
            normalise(ring[1], B - 1, B)
            variance(B - 1, B)
            finish(B - 1, B, 2)


_INS = ["x", "ctx_1024", "L0_xattn_W_qs", "L0_xattn_W_ks", "L0_xattn_W_vs", "L0_xattn_fc_w", "L0_xattn_fc_b",
        "L0_xattn_ln_g", "L0_xattn_ln_b"]


def kernel(**inputs):
    import numpy as _np
    import concourse.bacc as _bacc
    from concourse import mybir as _mybir
    from concourse.bass_utils import run_bass_kernel_spmd as _run

    nc = _bacc.Bacc("TRN2", target_bir_lowering=False, num_devices=1)
    arrays, args = {}, []
    for name in _INS:
        a = _np.ascontiguousarray(inputs[name])
        arrays[f"in_{name}_dram"] = a
        args.append(nc.dram_tensor(f"in_{name}_dram", a.shape, _mybir.dt.from_np(a.dtype), kind="ExternalInput").ap())
    shape = inputs["x"].shape
    args.append(nc.dram_tensor("out_0_dram", shape, _mybir.dt.float32, kind="ExternalOutput").ap())
    cross_attention(nc, *args)
    r = _run(nc, [arrays], core_ids=[0])
    return r.results[0]["out_0_dram"]
```

```python
from contextlib import ExitStack

import concourse.bass as bass
from concourse import mybir

F32 = mybir.dt.float32
F32R = mybir.dt.float32r
ALU = mybir.AluOpType
ACT = mybir.ActivationFunctionType
AX = mybir.AxisListType

P = 128
HEADS = 16
WARM_UP = 6
KD = 64
TEMPERATURE = float(KD) ** 0.5
LN_EPS = 1e-5

SLOTS = 12
CHUNKS = 3
CS = SLOTS // CHUNKS
QG = 4
RING = 5
TBANKS = 2
GROUPS = [range(0, 3), range(3, 6), range(6, 9), range(9, 13)]
NG = len(GROUPS)
PRODUCT_SLOTS = [4, 4, 4, 5, 3, 4, 4, 4, 4, 3, 3, 2, 4]

PROJ_STEP = 4
SIDE = {2: [("q", 0)], PROJ_STEP: [("proj", 0)], 5: [("ctxT", 0)], 6: [("q", 1)], 7: [("ctxT", 1)], 8: [("q", 2)],
        9: [("ctxT", 2)], 11: [("q", 3)]}
NEXT = ("q", "ctxT")
PREV = ("proj",)


def cross_attention(nc, x, ctx, w_q, w_k, w_v, fc_w, fc_b, ln_g, ln_b, out):
    B, Q, D = x.shape
    K = ctx.shape[1]
    V = fc_w.shape[1]
    ROWS = HEADS * Q
    TILES = -(-ROWS // P)
    PAIRS = HEADS * KD // P
    WHALF = HEADS * KD // 2
    FULL, REST = divmod(K, SLOTS)
    assert max(SIDE) < TILES - 1
    assert D == P and V == P and Q <= P and REST == CS and TILES == GROUPS[-1].stop

    def keys_on(c):
        return FULL + 1 if c == 0 else FULL

    WIDTH = [CS * keys_on(c) for c in range(CHUNKS)]
    START = [sum(WIDTH[:c]) for c in range(CHUNKS)]
    assert sum(WIDTH) == K and max(WIDTH) <= 512

    def rows(t):
        return min(P, ROWS - P * t)

    def group_of(t):
        return next(g for g in range(NG) if t in GROUPS[g])

    def group_rows(g):
        return sum(rows(t) for t in GROUPS[g])

    def ready_heads(g):
        return P * GROUPS[g].start // Q

    NC = CHUNKS * TILES
    QBLOCKS = HEADS // QG
    QB = QG * Q

    def q_block_of(t):
        return (P * t + rows(t) - 1) // QB

    def step_entries(t):
        return [("s", t + 1, c) for c in range(CHUNKS)] + [(kind, t, n) for kind, n in SIDE.get(t, [])]

    order = [e for t in range(TILES) for e in step_entries(t)]
    short = -len(order) % RING
    rounds = [RING - 1] * short + [RING] * ((len(order) - short * (RING - 1)) // RING)
    bank_of = dict(zip(order, [bank for r in rounds for bank in range(r)], strict=True))

    LAST_PROJ, LAST_PRODUCT = ("s", TILES, 0), ("s", TILES, 1)

    PV_BANK, T0_BANK, T1_BANK = RING, RING + 1, RING + 2
    early_bank = {("wqT", 0): T1_BANK, ("wkT", 0): 2, ("xT", 0): 3, ("A", 0): 0, ("A", 1): T0_BANK,
                  ("ctxT", 0): 1, ("ctxT", 1): 4, ("q", 0): 2, ("ctxT", 2): T1_BANK, ("wqT", 1): 3, ("wkT", 1): 0,
                  ("s", 0, 0): T0_BANK, ("s", 0, 1): 1, ("s", 0, 2): 4, ("A", 2): T1_BANK, ("A", 3): 2, ("q", 1): 3}
    early = list(early_bank)
    LATE = {(0, 0): ("q", 2), (0, 1): ("wvT", 0), (0, 2): ("wvT", 1), (1, 0): ("q", 3), (1, 1): ("M", 0),
            (1, 2): ("M", 1), (2, 0): ("M", 2), (2, 1): ("M", 3), (2, 2): ("xT", 1)}
    LATE_STEPS = GROUPS[0].stop
    BY_ACT = [("wkT", 0), ("A", 1), ("wkT", 1), ("A", 3), ("wvT", 0), ("M", 0), ("M", 3)]
    plain = [e for e in early + list(LATE.values()) if e[0] not in ("s", "q", "ctxT")]
    first_bank = dict(early_bank)
    for t in range(LATE_STEPS):
        for c in range(CHUNKS):
            n = CHUNKS * t + c
            first_bank["s", t + 1, c] = (0, 4, PV_BANK, 3)[n % 4]
            first_bank["t", t, c] = (T0_BANK, T1_BANK)[n % TBANKS]
            first_bank[LATE[t, c]] = (1, 2)[n % 2]
        for e in step_entries(t)[CHUNKS:]:
            if e[0] not in PREV:
                first_bank[e] = 4
    for e in [e for t in range(LATE_STEPS, TILES) for e in step_entries(t) if e[0] not in PREV]:
        first_bank[e] = bank_of[e]
    first_order = list(first_bank)

    PRODUCT, taken = {}, 0
    for t, count in enumerate(PRODUCT_SLOTS):
        PRODUCT[t] = range(taken % SLOTS, taken % SLOTS + count)
        taken += count
    assert all(sum(len(PRODUCT[t]) for t in group) == SLOTS for group in GROUPS)

    def filled(e):
        return plain.index(e) + 1

    with ExitStack() as stack:
        def sb(name, shape, dt=F32):
            return stack.enter_context(nc.sbuf_tensor(name, shape, dt))

        def sem(name):
            return stack.enter_context(nc.semaphore(name))

        ident = sb("ident", [P, P])
        zeros = sb("zeros", [P, P])
        one = sb("one", [P, 1, 1])
        ctx_in = sb("ctx_in", [P, SLOTS, P])
        ctx_hi = sb("ctx_hi", [P, SLOTS, P], F32R)
        ctx_lo = sb("ctx_lo", [P, SLOTS, P], F32R)
        ctxT_hi = sb("ctxT_hi", [P, 2, K], F32R)
        ctxT_lo = sb("ctxT_lo", [P, 2, K], F32R)
        q_hi = sb("q_hi", [P, TILES * P], F32R)
        q_lo = sb("q_lo", [P, TILES * P], F32R)
        weights = sb("weights", [P, 2, K])
        wt_hi = [sb(f"wt_hi{i}", [P, SLOTS, group_rows(2 + i)], F32R) for i in range(2)]
        wt_lo = [sb(f"wt_lo{i}", [P, SLOTS, group_rows(2 + i)], F32R) for i in range(2)]
        mx = sb("mx", [P, TILES, CHUNKS])
        neg_max = sb("neg_max", [P, TILES])
        row_sum = sb("row_sum", [P, TILES, CHUNKS])
        total = sb("total", [P, TILES])
        recip = sb("recip", [P, TILES])
        recip_rows = sb("recip_rows", [P, P * len(GROUPS[-1])])
        attended = sb("attended", [P, ROWS])
        A = sb("A", [P, HEADS, P])
        M = sb("M", [P, HEADS, P])
        xT = sb("xT", [P, B * Q])
        x_in = sb("x_in", [Q, B, P])
        x_res = sb("x_res", [Q, B, P])
        w_in = sb("w_in", [P, HEADS * KD])
        wk_in = sb("wk_in", [P, HEADS * KD])
        wT = sb("wT", [P, PAIRS, P])
        wkT = sb("wkT", [P, PAIRS, P])
        fc_in = sb("fc_in", [P, PAIRS, P])
        rows_in = sb("rows_in", [Q, 3, P])
        y = sb("y", [Q, P])
        y_sum, neg_mean, squares = sb("y_sum", [Q, 1]), sb("neg_mean", [Q, 1]), sb("squares", [Q, 1])
        squared = sb("squared", [Q, P])
        z = sb("z", [Q, B, P])
        var = sb("var", [Q, B])
        std = sb("std", [Q, B])
        rstd = sb("rstd", [Q, B])

        recip_line = nc.dram_tensor("recip_line", [NG, P * len(GROUPS[-1])], F32, kind="Internal").ap()

        ring = [stack.enter_context(nc.psum_tensor(f"ring{i}", [P, 512], F32)) for i in range(RING)]
        tbank = [stack.enter_context(nc.psum_tensor(f"tbank{i}", [P, CS, P], F32)) for i in range(TBANKS)]
        pv = stack.enter_context(nc.psum_tensor("pv", [P, 512], F32))
        banks = ring + [pv] + [bank[:, :, :].rearrange("p s r -> p (s r)") for bank in tbank]

        ident_zeroed, ident_ready = sem("ident_zeroed"), sem("ident_ready")
        filler_set = sem("filler_set")
        x_loaded, wv_loaded = sem("x_loaded"), sem("wv_loaded")
        wq_loaded = [sem(f"wq_loaded{i}") for i in range(2)]
        wk_loaded = [sem(f"wk_loaded{i}") for i in range(2)]
        fc_loaded, rows_loaded, ctx_loaded = sem("fc_loaded"), sem("rows_loaded"), sem("ctx_loaded")
        zeros_set = sem("zeros_set")
        start_filled = sem("start_filled")
        start_copied, start_copied_act = sem("start_copied"), sem("start_copied_act")
        x_res_ready = sem("x_res_ready")
        scores_ready = sem("scores_ready")
        chunk_max = sem("chunk_max")
        max_ready = sem("max_ready")
        exp_done = sem("exp_done")
        wt_ready = sem("wt_ready")
        wt_hi_done = sem("wt_hi_done")
        wt_lo_done = sem("wt_lo_done")
        pv_done = sem("pv_done")
        total_ready = sem("total_ready")
        recip_ready = sem("recip_ready")
        recip_stored = sem("recip_stored")
        rows_spread = sem("rows_spread")
        attended_done = sem("attended_done")
        q_ready, q_hi_done, q_lo_done = sem("q_ready"), sem("q_hi_done"), sem("q_lo_done")
        ctxT_ready, ctxT_hi_done, ctxT_lo_done = sem("ctxT_ready"), sem("ctxT_hi_done"), sem("ctxT_lo_done")
        ctx_hi_done, ctx_lo_done = sem("ctx_hi_done"), sem("ctx_lo_done")
        proj_ready = sem("proj_ready")
        y_ready, mean_ready = sem("y_ready"), sem("mean_ready")
        squares_ready, z_ready = sem("squares_ready"), sem("z_ready")
        var_ready, std_ready, rstd_ready = sem("var_ready"), sem("std_ready"), sem("rstd_ready")
        result_ready, stored = sem("result_ready"), sem("stored")

        def batches(eng, body):
            body(0, True, False)
            with eng.Fori(1, B - 1) as b:
                body(b, False, False)
            body(B - 1, False, True)

        def in_this_batch(kind, first, last):
            return not (first and kind in PREV) and not (last and kind in NEXT)

        def side_work(t, first, last):
            return [(kind, n) for kind, n in SIDE.get(t, []) if in_this_batch(kind, first, last)]

        def there(e, first, last):
            if e[0] == "s":
                return not (last and e[1] == TILES)
            return in_this_batch(e[0], first, last)

        def read_out(e, b):
            kind, t, n = e
            if kind == "s":
                return exp_done, b * NC + (CHUNKS * t + n + 1)
            if kind == "q":
                return q_lo_done, b * QBLOCKS + (QBLOCKS + n + 1)
            if kind == "ctxT":
                return ctxT_lo_done, b * CHUNKS + (CHUNKS + n + 1)
            return y_ready, b

        def copied(e):
            by_act = e in BY_ACT
            mine = [f for f in plain if (f in BY_ACT) == by_act]
            return (start_copied_act if by_act else start_copied), mine.index(e) + 1

        def start_read_out(e):
            if e[0] in ("s", "q", "ctxT"):
                n = CHUNKS * e[1] + e[2] if e[0] == "s" else e[1]
                return {"s": exp_done, "q": q_lo_done, "ctxT": ctxT_lo_done}[e[0]], n + 1
            return copied(e)

        def bank(e, first):
            return banks[first_bank[e] if first else bank_of[e]]

        def bank_free(e, b, first, last):
            if first:
                before = [f for f in first_order[:first_order.index(e)] if first_bank[f] == first_bank[e]]
                if not before:
                    return None
                f = before[-1]
                return start_read_out(f) if len(f) == 2 or f[0] == "s" else read_out(f, b)
            before = [f for f in order[:order.index(e)] if bank_of[f] == bank_of[e] and there(f, first, last)]
            if before:
                return read_out(before[-1], b)
            return read_out([f for f in order if bank_of[f] == bank_of[e]][-1], b - 1)

        def place(e):
            kind, n = e
            if kind in ("A", "M"):
                h = 8 * (n // 2) + n % 2
                heads = slice(h, h + 7, 2)
                return (A[:, heads, :], 1.0 / TEMPERATURE) if kind == "A" else (M[:, heads, :], 1.0)
            return (wkT if kind == "wkT" else wT)[:, 4 * n:4 * n + 4, :], 1.0

        block = stack.enter_context(nc.Block())

        def load_ctx(sp, b):
            sp.dma_start(ctx_in[0:FULL, :, :],
                         ctx[b, 0:SLOTS * FULL, :].rearrange("(p s) d -> p s d", s=SLOTS)).then_inc(ctx_loaded, 16)
            sp.dma_start(ctx_in[FULL:FULL + 1, 0:CS, :],
                         ctx[b, SLOTS * FULL:K, :].rearrange("(p s) d -> p s d", s=CS)).then_inc(ctx_loaded, 16)

        @block.sync
        def _(sp):
            sp.dma_start(w_in[:, 0:WHALF], w_q[:, 0:WHALF]).then_inc(wq_loaded[0], 16)
            sp.dma_start(x_in[:, :, :], x.rearrange("b q d -> q b d")).then_inc(x_loaded, 16)
            sp.dma_start(w_in[:, WHALF:], w_q[:, WHALF:]).then_inc(wq_loaded[1], 16)
            sp.dma_start(fc_in[:, :, :], fc_w.rearrange("(n p) d -> p n d", p=P)).then_inc(fc_loaded, 16)
            for n, row in enumerate((fc_b, ln_g, ln_b)):
                sp.dma_start(rows_in[:, n, :], row.rearrange("(a d) -> a d", a=1).broadcast_to([Q, P]))\
                  .then_inc(rows_loaded, 16)
            sp.wait_ge(start_filled, filled(("wqT", 1)))
            sp.dma_start(w_in[:, :], w_v).then_inc(wv_loaded, 16)

            def spread_reciprocals(b, g, first):
                n = len(GROUPS[g])
                sp.wait_ge(recip_ready, b * NG + g + 1)
                sp.dma_start(recip_line[g, 0:P * n].rearrange("(p t) -> p t", t=n),
                             recip[:, GROUPS[g].start:GROUPS[g].stop]).then_inc(recip_stored, 16)
                sp.wait_ge(recip_stored, b * 16 * NG + 16 * (g + 1))
                if not (first and g == 0):
                    sp.wait_ge(attended_done, b * NG + g)
                sp.dma_start(recip_rows[:, 0:P * n], recip_line[g:g + 1, 0:P * n].broadcast_to([P, P * n]))\
                  .then_inc(rows_spread, 16)

            def body(b, first, last):
                if not last:
                    sp.wait_ge(ctx_lo_done, b * CHUNKS + CHUNKS)
                    sp.wait_ge(ctxT_ready, b * CHUNKS + CHUNKS)
                    load_ctx(sp, b + 1)
                for g in range(NG):
                    spread_reciprocals(b, g, first)
            batches(sp, body)

            sp.wait_ge(result_ready, B - 1)
            sp.dma_start(out[0:B - 1].rearrange("b q d -> q b d"), z[:, 0:B - 1, :]).then_inc(stored, 16)
            sp.wait_ge(result_ready, B)
            sp.dma_start(out[B - 1], z[:, B - 1, :]).then_inc(stored, 16)
            sp.wait_ge(stored, 32)

        @block.gpsimd
        def _(pool):
            pool.memset(ident[:, :], 0.0).then_inc(ident_zeroed, 1)
            pool.wait_ge(ident_zeroed, 1)
            pool.affine_select(out=ident[:, :], in_=ident[:, :], compare_op=ALU.not_equal, fill=1.0, base=0,
                               pattern=[[-1, P]], channel_multiplier=1).then_inc(ident_ready, 1)
            pool.memset(one[:, :, :], 1.0).then_inc(filler_set, 1)
            for part in (q_hi, q_lo):
                pool.memset(part[:, ROWS:TILES * P].bitcast(F32), 0.0).then_inc(filler_set, 1)

            def body(b, first, last):
                if first:
                    pool.wait_ge(filler_set, 1)
                pool.wait_ge(ctx_loaded, b * 32 + 32)
                for c in range(CHUNKS):
                    part = (slice(0, keys_on(c)), slice(CS * c, CS * c + CS))
                    if not first:
                        pool.wait_ge(pv_done, b * NG * CHUNKS + (c + 1 - CHUNKS))
                    pool.tensor_tensor(ctx_hi[part], ctx_in[part],
                                       one[0:keys_on(c), :, :].broadcast_to([keys_on(c), CS, P]), ALU.mult)\
                        .then_inc(ctx_hi_done, 1)
                    pool.wait_ge(ctx_hi_done, b * CHUNKS + c + 1)
                    pool.tensor_tensor(ctx_lo[part], ctx_in[part], ctx_hi[part].bitcast(F32), ALU.subtract)\
                        .then_inc(ctx_lo_done, 1)
                if first:
                    pool.wait_ge(x_loaded, 16)
                    pool.wait_ge(rows_loaded, 48)
                    pool.tensor_tensor(x_res[:, :, :], x_in[:, :, :],
                                       rows_in[:, 0:1, :].broadcast_to([Q, B, P]), ALU.add).then_inc(x_res_ready, 1)
            batches(pool, body)

        @block.tensor
        def _(pe):
            def wait_for_bank(e, b, first, last):
                free = bank_free(e, b, first, last)
                if free:
                    pe.wait_ge(*free)

            def scores(dst, parity, t, c):
                lhs = slice(P * t, P * t + P)
                keys = slice(START[c], START[c] + WIDTH[c])
                o = dst[:, 0:WIDTH[c]]
                pe.matmul(o, q_hi[:, lhs], ctxT_hi[:, parity, keys], start=True, stop=False)
                pe.matmul(o, q_hi[:, lhs], ctxT_lo[:, parity, keys], start=False, stop=False)
                pe.matmul(o, q_lo[:, lhs], ctxT_hi[:, parity, keys], start=False, stop=True).then_inc(scores_ready, 1)

            def transpose_ctx(dst, c):
                n = keys_on(c)
                for i in range(CS):
                    last = pe.transpose(dst[:, n * i:n * i + n], ctx_in[0:n, CS * c + i, :], ident[0:n, 0:n])
                last.then_inc(ctxT_ready, 1)

            def project_queries(dst, b, n):
                for i in range(QG):
                    last = pe.matmul(dst[:, Q * i:Q * i + Q], A[:, QG * n + i, :], xT[:, bass.ds(b * Q, Q)],
                                     start=True, stop=True)
                last.then_inc(q_ready, 1)

            def transpose_w(dst, source, n):
                for i in range(4):
                    pair = 4 * n + i
                    last = pe.transpose(dst[:, P * i:P * i + P], source[:, P * pair:P * pair + P], ident[:, :])
                return last

            def merge(dst, right, n):
                for i in range(4):
                    h = 8 * (n // 2) + 2 * i + n % 2
                    half = slice(KD * (h % 2), KD * (h % 2) + KD)
                    last = pe.matmul(dst[:, P * i:P * i + P], wT[half, h // 2, :], right[half, h // 2, :],
                                     start=True, stop=True)
                return last

            def start(e):
                dst = banks[first_bank[e]]
                wait_for_bank(e, 0, True, False)
                kind, n = e[0], e[1]
                if kind == "xT":
                    pe.wait_ge(x_loaded, 16)
                    for i in range(B // 2):
                        done = pe.transpose(dst[:, Q * i:Q * i + Q], x_in[:, B // 2 * n + i, :], ident[0:Q, 0:Q])
                elif kind in ("wqT", "wkT", "wvT"):
                    if kind == "wvT":
                        pe.wait_ge(wv_loaded, 16)
                    else:
                        pe.wait_ge((wq_loaded if kind == "wqT" else wk_loaded)[n], 16)
                    done = transpose_w(dst, wk_in if kind == "wkT" else w_in, n)
                elif kind == "A":
                    pe.wait_ge(*copied(("wqT", n // 2)))
                    pe.wait_ge(*copied(("wkT", n // 2)))
                    done = merge(dst, wkT, n)
                elif kind == "M":
                    pe.wait_ge(fc_loaded, 16)
                    pe.wait_ge(*copied(("wvT", n // 2)))
                    done = merge(dst, fc_in, n)
                elif kind == "ctxT":
                    pe.wait_ge(ctx_loaded, 32)
                    transpose_ctx(dst, n)
                elif kind == "q":
                    pe.wait_ge(*copied(("xT", 0)))
                    pe.wait_ge(*copied(("A", 2 * (n // 2))))
                    pe.wait_ge(*copied(("A", 2 * (n // 2) + 1)))
                    project_queries(dst, 0, n)
                else:
                    pe.wait_ge(ctxT_lo_done, e[2] + 1)
                    pe.wait_ge(q_lo_done, 1)
                    pe.wait_ge(filler_set, 3)
                    scores(dst, 0, 0, e[2])
                if kind not in ("ctxT", "q", "s"):
                    done.then_inc(start_filled, 1)

            pe.wait_ge(zeros_set, 1)
            for _ in range(WARM_UP):
                pe.matmul(pv[:, 0:P], zeros[:, :], zeros[:, :], start=True, stop=True)
            pe.wait_ge(ident_ready, 1)
            for e in early:
                start(e)

            def body(b, first, last):
                def next_scores(t, c):
                    e = ("s", t + 1, c)
                    dst = bank(e, first)
                    ahead = t == TILES - 1
                    tile, at = (0, b + 1) if ahead else (t + 1, b)
                    if c == 0 and (tile == 0 or q_block_of(tile) > q_block_of(tile - 1)):
                        pe.wait_ge(q_lo_done, at * QBLOCKS + q_block_of(tile) + 1)
                    if ahead:
                        pe.wait_ge(ctxT_lo_done, at * CHUNKS + c + 1)
                    wait_for_bank(e, b, first, last)
                    scores(dst, at % 2, tile, c)

                def transpose_weights(t, c):
                    k = CHUNKS * t + c
                    n = keys_on(c)
                    dst = tbank[k % TBANKS]
                    pe.wait_ge(exp_done, b * NC + k + 1)
                    if first and k < TBANKS:
                        wait_for_bank(("t", t, c), b, first, last)
                    else:
                        pe.wait_ge(wt_lo_done, b * NC + (k - TBANKS + 1 if k >= TBANKS else -((NC - 1 - k) % TBANKS)))
                    for i in range(CS):
                        at = START[c] + n * i
                        r = rows(t) if i else P
                        done = pe.transpose(dst[0:n, i, 0:r], weights[0:r, t % 2, at:at + n], ident[0:r, 0:r])
                    done.then_inc(wt_ready, 1)

                def side(t, kind, n):
                    dst = bank((kind, t, n), first)
                    wait_for_bank((kind, t, n), b, first, last)
                    if kind == "q":
                        project_queries(dst, b + 1, n)
                    elif kind == "ctxT":
                        pe.wait_ge(ctx_loaded, b * 32 + 64)
                        transpose_ctx(dst, n)
                    else:
                        pe.wait_ge(attended_done, b * NG)
                        project_out(dst, 0, HEADS)

                def context_product(t, part=None):
                    g = group_of(t)
                    if first and g == 0:
                        return
                    slots = PRODUCT[t]
                    if part is not None:
                        slots = slots[len(slots) * part // CHUNKS:len(slots) * (part + 1) // CHUNKS]
                    for s in slots:
                        c = s // CS
                        if s % CS == 0:
                            if g == 1:
                                pe.wait_ge(ctx_lo_done, b * CHUNKS + c + 1)
                            pe.wait_ge(wt_lo_done, b * NC + CHUNKS * (GROUPS[g].start - 1) + c + 1)
                        if s == 0 and first and g == 1:
                            pe.wait_ge(*start_read_out([e for e in first_order if first_bank[e] == PV_BANK][-1]))
                        elif s == 0:
                            pe.wait_ge(attended_done, b * NG + g - 1)
                        product(g - 1 if g else NG - 1, s)

                for t in range(TILES):
                    ahead = not (last and t == TILES - 1)
                    for c in range(CHUNKS):
                        if ahead:
                            next_scores(t, c)
                        elif c != 1:
                            if c == 0:
                                wait_for_bank(LAST_PROJ, b, first, last)
                                pe.wait_ge(attended_done, b * NG + 2)
                            project_out(bank(LAST_PROJ, first), *((0, 3) if c == 0 else (3, ready_heads(2))))
                        transpose_weights(t, c)
                        if first and t < LATE_STEPS:
                            start(LATE[t, c])
                        if not ahead:
                            context_product(t, c)
                    for kind, n in side_work(t, first, last):
                        side(t, kind, n)
                    if ahead:
                        context_product(t)

            def product(g, s, pv=pv):
                n = keys_on(s // CS)
                w = group_rows(g)
                hi, lo = wt_hi[g % 2][0:n, s, 0:w], wt_lo[g % 2][0:n, s, 0:w]
                pe.matmul(pv[:, 0:w], ctx_hi[0:n, s, :], hi, start=(s == 0), stop=False)
                pe.matmul(pv[:, 0:w], ctx_lo[0:n, s, :], hi, start=False, stop=False)
                done = pe.matmul(pv[:, 0:w], ctx_hi[0:n, s, :], lo, start=False, stop=(s == SLOTS - 1))
                if s % CS == CS - 1:
                    done.then_inc(pv_done, 1)

            def project_out(dst, h0, h1):
                for h in range(h0, h1):
                    done = pe.matmul(dst[0:Q, 0:V], attended[:, Q * h:Q * h + Q], M[:, h, :],
                                     start=(h == 0), stop=(h == HEADS - 1))
                if h1 == HEADS:
                    done.then_inc(proj_ready, 1)

            batches(pe, body)

            for c in range(CHUNKS):
                if c == 0:
                    wait_for_bank(LAST_PRODUCT, B - 1, False, True)
                pe.wait_ge(wt_lo_done, B * NC - CHUNKS + c + 1)
                for s in range(CS * c, CS * c + CS):
                    product(NG - 1, s, bank(LAST_PRODUCT, False))
            pe.wait_ge(attended_done, B * NG - 1)
            project_out(bank(LAST_PROJ, False), ready_heads(2), ready_heads(3))
            pe.wait_ge(attended_done, B * NG)
            project_out(bank(LAST_PROJ, False), ready_heads(3), HEADS)

        @block.scalar
        def _(act):
            act.dma_start(wk_in[:, 0:WHALF], w_k[:, 0:WHALF]).then_inc(wk_loaded[0], 16)
            load_ctx(act, 0)
            act.dma_start(wk_in[:, WHALF:], w_k[:, WHALF:]).then_inc(wk_loaded[1], 16)

            def exp_chunk(src, b, t, c):
                act.activation(weights[:, t % 2, START[c]:START[c] + WIDTH[c]], src[:, 0:WIDTH[c]], ACT.Exp,
                               bias=neg_max[:, t:t + 1], accum_out=row_sum[:, t, c:c + 1]).then_inc(exp_done, 1)

            def q_high(src, b, n):
                act.wait_ge(q_ready, b * QBLOCKS + n + 1)
                act.activation(q_hi[:, QB * n:QB * n + QB], src[:, 0:QB], ACT.Copy).then_inc(q_hi_done, 1)

            def ctxT_high(src, b, c):
                act.wait_ge(ctxT_ready, b * CHUNKS + c + 1)
                act.activation(ctxT_hi[:, b % 2, START[c]:START[c] + WIDTH[c]], src[:, 0:WIDTH[c]], ACT.Copy)\
                   .then_inc(ctxT_hi_done, 1)

            def start(e):
                src = banks[first_bank[e]]
                if e[0] == "q":
                    q_high(src, 0, e[1])
                elif e[0] == "ctxT":
                    ctxT_high(src, 0, e[1])
                elif e[0] == "s":
                    if e[2] == 0:
                        act.wait_ge(max_ready, 1)
                    exp_chunk(src, 0, 0, e[2])
                elif e in BY_ACT:
                    act.wait_ge(start_filled, filled(e))
                    dst, scale = place(e)
                    act.activation(dst, src[:, :].rearrange("p (h d) -> p h d", h=4), ACT.Copy, scale=scale)\
                        .then_inc(start_copied_act, 1)

            for e in early:
                start(e)

            def sum_squares(count):
                act.wait_ge(mean_ready, count)
                act.activation(squared[:, :], y[:, :], ACT.Square, bias=neg_mean[:, 0:1], accum_out=squares[:, :])\
                   .then_inc(squares_ready, 1)

            def side(b, t, first, last):
                if t == PROJ_STEP + 1 and not first:
                    sum_squares(b)
                for kind, n in side_work(t, first, last):
                    src = bank((kind, t, n), first)
                    if kind == "q":
                        q_high(src, b + 1, n)
                    elif kind == "ctxT":
                        ctxT_high(src, b + 1, n)

            def body(b, first, last):
                for t in range(TILES):
                    g = group_of(t)
                    r = rows(t)
                    at = P * (t - GROUPS[g].start)
                    for c in range(CHUNKS):
                        k = CHUNKS * t + c
                        n = keys_on(c)
                        if t == GROUPS[g].start and not (first and g < 2):
                            act.wait_ge(pv_done, (b * NG + (g - 2)) * CHUNKS + c + 1)
                        act.wait_ge(wt_ready, b * NC + k + 1)
                        act.activation(wt_hi[g % 2][0:n, CS * c:CS * c + CS, at:at + r],
                                       tbank[k % TBANKS][0:n, :, 0:r], ACT.Copy).then_inc(wt_hi_done, 1)
                        if first and t < LATE_STEPS and c < CHUNKS - 1:
                            start(LATE[t, c])
                    if not (last and t == TILES - 1):
                        tile, bb = (0, b + 1) if t == TILES - 1 else (t + 1, b)
                        act.wait_ge(max_ready, bb * TILES + tile + 1)
                        for c in range(CHUNKS):
                            e = ("s", t + 1, c)
                            src = bank(e, first)
                            if tile == 0:
                                act.wait_ge(wt_ready, bb * NC + (c + 1 - CHUNKS))
                            exp_chunk(src, bb, tile, c)
                    if first and t < LATE_STEPS:
                        start(LATE[t, CHUNKS - 1])
                    side(b, t, first, last)
            batches(act, body)

            act.wait_ge(var_ready, B - 1)
            act.activation(std[:, 0:B - 1], var[:, 0:B - 1], ACT.Sqrt).then_inc(std_ready, 1)
            sum_squares(B)
            act.wait_ge(var_ready, B)
            act.activation(std[:, B - 1:B], var[:, B - 1:B], ACT.Sqrt).then_inc(std_ready, 1)

        @block.vector
        def _(dve):
            def chunk_maximum(src, b, t, c):
                dve.wait_ge(scores_ready, b * NC + (CHUNKS * t + c + 1))
                dve.tensor_reduce(mx[:, t, c:c + 1], src[:, 0:WIDTH[c]], AX.X, ALU.max).then_inc(chunk_max, 1)

            def tile_maximum(b, t):
                dve.wait_ge(chunk_max, b * NC + CHUNKS * (t + 1))
                dve.tensor_reduce(neg_max[:, t:t + 1], mx[:, t, :], AX.X, ALU.max, negate=True)\
                   .then_inc(max_ready, 1)

            def q_low(src, b, n):
                part = slice(QB * n, QB * n + QB)
                dve.wait_ge(q_hi_done, b * QBLOCKS + n + 1)
                dve.tensor_tensor(q_lo[:, part], src[:, 0:QB], q_hi[:, part].bitcast(F32), ALU.subtract)\
                   .then_inc(q_lo_done, 1)

            def ctxT_low(src, b, c):
                part = slice(START[c], START[c] + WIDTH[c])
                dve.wait_ge(ctxT_hi_done, b * CHUNKS + c + 1)
                dve.tensor_tensor(ctxT_lo[:, b % 2, part], src[:, 0:WIDTH[c]],
                                  ctxT_hi[:, b % 2, part].bitcast(F32), ALU.subtract).then_inc(ctxT_lo_done, 1)

            def attend(b, g, pv=pv):
                w = group_rows(g)
                at = P * GROUPS[g].start
                dve.wait_ge(rows_spread, b * NG * 16 + (g + 1) * 16)
                dve.wait_ge(pv_done, (b * NG + g) * CHUNKS + CHUNKS)
                n = len(GROUPS[g])
                by_tile = recip_rows[:, 0:P * n].rearrange("p (r t) -> p t r", t=n)
                full = w // P
                done = dve.tensor_tensor(attended[:, at:at + P * full].rearrange("p (t r) -> p t r", t=full),
                                         pv[:, 0:P * full].rearrange("p (t r) -> p t r", t=full),
                                         by_tile[:, 0:full, :], ALU.mult)
                if w > P * full:
                    done = dve.tensor_tensor(attended[:, at + P * full:at + w], pv[:, P * full:w],
                                             by_tile[:, full, 0:w - P * full], ALU.mult)
                done.then_inc(attended_done, 1)

            def normalise(src, b, count):
                dve.wait_ge(proj_ready, count)
                dve.scalar_tensor_tensor(y[:, :], src[0:Q, 0:V], 1.0, x_res[:, b, :], ALU.mult, ALU.add,
                                         accum_out=y_sum[:, :]).then_inc(y_ready, 1)
                dve.wait_ge(y_ready, count)
                dve.tensor_scalar(neg_mean[:, :], y_sum[:, :], -1.0 / V, None, ALU.mult).then_inc(mean_ready, 1)
                dve.wait_ge(mean_ready, count)
                dve.scalar_tensor_tensor(z[:, b, :], y[:, :], neg_mean[:, 0:1], rows_in[:, 1, :], ALU.add, ALU.mult)\
                   .then_inc(z_ready, 1)

            def variance(b, count):
                dve.wait_ge(squares_ready, count)
                dve.tensor_scalar(var[:, bass.ds(b, 1)], squares[:, :], 1.0 / V, LN_EPS, ALU.mult, ALU.add)\
                   .then_inc(var_ready, 1)

            def start(e):
                src = banks[first_bank[e]]
                if e[0] == "q":
                    q_low(src, 0, e[1])
                elif e[0] == "ctxT":
                    ctxT_low(src, 0, e[1])
                elif e[0] == "s":
                    chunk_maximum(src, 0, 0, e[2])
                    if e[2] == CHUNKS - 1:
                        tile_maximum(0, 0)
                elif e not in BY_ACT:
                    dve.wait_ge(start_filled, filled(e))
                    if e[0] == "xT":
                        w = B // 2 * Q
                        copy = dve.tensor_copy(xT[:, w * e[1]:w * e[1] + w], src[:, 0:w])
                    else:
                        dst, scale = place(e)
                        copy = dve.tensor_scalar(dst, src[:, :].rearrange("p (h d) -> p h d", h=4), scale, None,
                                                 ALU.mult)
                    copy.then_inc(start_copied, 1)

            dve.memset(zeros[:, :], 0.0).then_inc(zeros_set, 1)
            for e in early:
                start(e)

            def step_before(b, t, first, last):
                for kind, n in side_work(t, first, last):
                    src = bank((kind, t, n), first)
                    if kind == "q":
                        q_low(src, b + 1, n)
                    elif kind == "ctxT":
                        ctxT_low(src, b + 1, n)
                    else:
                        normalise(src, b - 1, b)

            def body(b, first, last):
                for t in range(TILES):
                    g = group_of(t)
                    r = rows(t)
                    at = P * (t - GROUPS[g].start)

                    def next_maximum(c):
                        if last and t == TILES - 1:
                            return
                        tile, bb = (0, b + 1) if t == TILES - 1 else (t + 1, b)
                        chunk_maximum(bank(("s", t + 1, c), first), bb, tile, c)
                        if c == CHUNKS - 1:
                            tile_maximum(bb, tile)

                    def low_half(c):
                        k = CHUNKS * t + c
                        n = keys_on(c)
                        hi = wt_hi[g % 2][0:n, CS * c:CS * c + CS, at:at + r]
                        dve.wait_ge(wt_hi_done, b * NC + k + 1)
                        dve.tensor_tensor(wt_lo[g % 2][0:n, CS * c:CS * c + CS, at:at + r],
                                          tbank[k % TBANKS][0:n, :, 0:r], hi.bitcast(F32), ALU.subtract)\
                           .then_inc(wt_lo_done, 1)

                    if t == GROUPS[g].start:
                        if g > 1:
                            attend(b, g - 2)
                        elif not first:
                            attend(b - 1, g + NG - 2)

                    next_maximum(0)
                    if t == PROJ_STEP + 2 and not first:
                        variance(b - 1, b)
                    low_half(0)
                    next_maximum(1)
                    if first and t < LATE_STEPS:
                        start(LATE[t, 0])
                    next_maximum(2)
                    low_half(1)
                    if first and t < LATE_STEPS:
                        start(LATE[t, 1])
                    step_before(b, t - 1, first, last)
                    low_half(2)
                    if first and t < LATE_STEPS:
                        start(LATE[t, CHUNKS - 1])
                    if t == GROUPS[g].stop - 1:
                        tiles = slice(GROUPS[g].start, GROUPS[g].stop)
                        dve.wait_ge(exp_done, b * NC + CHUNKS * GROUPS[g].stop)
                        dve.tensor_reduce(total[:, tiles], row_sum[:, tiles, :], AX.X, ALU.add).then_inc(total_ready, 1)
                        dve.wait_ge(total_ready, b * NG + g + 1)
                        dve.reciprocal(recip[:, tiles], total[:, tiles]).then_inc(recip_ready, 1)
                if first:
                    dve.wait_ge(x_res_ready, 1)
            batches(dve, body)

            def finish(b0, b1, count):
                dve.wait_ge(std_ready, count)
                dve.reciprocal(rstd[:, b0:b1], std[:, b0:b1]).then_inc(rstd_ready, 1)
                dve.wait_ge(rstd_ready, count)
                dve.wait_ge(z_ready, b1)
                for b in range(b0, b1):
                    dve.scalar_tensor_tensor(z[:, b, :], z[:, b, :], rstd[:, b:b + 1], rows_in[:, 2, :],
                                             ALU.mult, ALU.add).then_inc(result_ready, 1)

            attend(B - 1, NG - 2)
            finish(0, B - 1, 1)
            attend(B - 1, NG - 1, bank(LAST_PRODUCT, False))
            normalise(bank(LAST_PROJ, False), B - 1, B)
            variance(B - 1, B)
            finish(B - 1, B, 2)


_INS = ["x", "ctx_1024", "L0_xattn_W_qs", "L0_xattn_W_ks", "L0_xattn_W_vs", "L0_xattn_fc_w", "L0_xattn_fc_b",
        "L0_xattn_ln_g", "L0_xattn_ln_b"]


def kernel(**inputs):
    import numpy as _np
    import concourse.bacc as _bacc
    from concourse import mybir as _mybir
    from concourse.bass_utils import run_bass_kernel_spmd as _run

    nc = _bacc.Bacc("TRN2", target_bir_lowering=False, num_devices=1)
    arrays, args = {}, []
    for name in _INS:
        a = _np.ascontiguousarray(inputs[name])
        arrays[f"in_{name}_dram"] = a
        args.append(nc.dram_tensor(f"in_{name}_dram", a.shape, _mybir.dt.from_np(a.dtype), kind="ExternalInput").ap())
    shape = inputs["x"].shape
    args.append(nc.dram_tensor("out_0_dram", shape, _mybir.dt.float32, kind="ExternalOutput").ap())
    cross_attention(nc, *args)
    r = _run(nc, [arrays], core_ids=[0])
    return r.results[0]["out_0_dram"]
```
